# Optimizing a Trainium2 kernel written in Bass

```python
import numpy as np
import jax
import jax.numpy as jnp

def _softmax(x, axis=-1):
    return jax.nn.softmax(x, axis=axis)

def _gelu(x):
    return jax.nn.gelu(x, approximate=True)

def _silu(x):
    return jax.nn.silu(x)

def _sigmoid(x):
    return jax.nn.sigmoid(x)

def _layernorm(x, axis=-1, eps=1e-05):
    m = jnp.mean(x, axis=axis, keepdims=True)
    v = jnp.var(x, axis=axis, keepdims=True)
    return (x - m) / jnp.sqrt(v + eps)

def _scatter_add(tgt, idx, src, axis=0):
    return tgt.at[idx].add(src)

def _segment_sum(src, seg, n):
    return jax.ops.segment_sum(src, seg, n)
kernel_name = 'mk_adaln_ffn_d1_seqx_r2_eceb5f'

def setup_inputs(seed: int=0):
    np.random.seed(seed)
    _w = jnp.asarray

    def _rec_inputs():
        import jax
        import jax.numpy as jnp
        _rk = jax.random.key(seed)
        x = -0.000125 + 0.9999 * jax.random.normal(jax.random.fold_in(_rk, 1), (8, 512, 2048), jnp.float32)
        _lenS = 512 - jax.random.randint(jax.random.fold_in(_rk, 7), (8,), 0, max(1, 512 // 4) + 1, jnp.int32)
        _lenS2 = 512 - jax.random.randint(jax.random.fold_in(_rk, 8), (8,), 0, max(1, 512 // 4) + 1, jnp.int32)
        itok_B_3_7 = jax.random.randint(jax.random.fold_in(_rk, 11), (8,), 3, 8, jnp.int32)
        return (x, itok_B_3_7)
    x, itok_B_3_7 = _rec_inputs()

    def _L0_cond_setup():
        import jax, jax.numpy as jnp
        import numpy as np
        MAX_LORAS, OUT, IN = (8, 2048, 2048)
        B, S = (4, 1024)
        key = jax.random.key(seed)
        k1, k2, k3 = jax.random.split(key, 3)
        x = jax.random.normal(k1, (B, S, IN), dtype=jnp.float32)
        weight = jax.random.normal(k2, (MAX_LORAS, OUT, IN), dtype=jnp.float32) * 0.02
        adapter_ids = jax.random.randint(k3, (B,), 0, MAX_LORAS, dtype=jnp.int32)
        return {'x': x, 'weight': weight, 'adapter_ids': adapter_ids}
    _L0_cond_all = _L0_cond_setup()
    _L0_cond_in = {k: v for k, v in _L0_cond_all.items() if k in ('weight',)}
    del _L0_cond_all

    def _L0_ffn_setup():
        import jax, jax.numpy as jnp
        import numpy as np
        N_STREAMS = 4
        DIM = 512
        SINKHORN_ITERS = 50
        SINKHORN_TAU = 0.1
        RMS_EPS = 1.1920929e-07

        def sinkhorn_log(logits, num_iters=SINKHORN_ITERS, tau=SINKHORN_TAU):
            Z = logits / tau
            u0 = jnp.zeros(Z.shape[:-1], Z.dtype)
            v0 = jnp.zeros_like(u0)

            def step(carry, _):
                u, v = carry
                u = -jax.nn.logsumexp(Z + v[..., None, :], axis=-1)
                v = -jax.nn.logsumexp(Z + u[..., :, None], axis=-2)
                return ((u, v), None)
            (u, v), _ = jax.lax.scan(step, (u0, v0), None, length=num_iters)
            return jnp.exp(Z + u[..., :, None] + v[..., None, :])
        key = jax.random.key(seed)
        ks = jax.random.split(key, 6)
        B, T = (4, 1024)
        n, C = (N_STREAMS, DIM)
        wd = n * C
        x = jax.random.normal(ks[0], (B, T, wd), dtype=jnp.float32)
        W_res = 0.01 * jax.random.normal(ks[1], (n * n, wd), dtype=jnp.float32)
        W_pre = 0.01 * jax.random.normal(ks[2], (n, wd), dtype=jnp.float32)
        W_post = 0.01 * jax.random.normal(ks[3], (n, wd), dtype=jnp.float32)
        H_res_base = jnp.full((n, n), -0.5, dtype=jnp.float32)
        H_res_base = H_res_base.at[jnp.arange(n), jnp.arange(n)].set(0.0)
        H_pre_base = jnp.zeros((n,), dtype=jnp.float32).at[0].set(1.0)
        H_post_base = jnp.zeros((n,), dtype=jnp.float32)
        gate = jnp.array([5.0], dtype=jnp.float32)
        W_branch = 1.0 / np.sqrt(C) * jax.random.normal(ks[4], (C, C), dtype=jnp.float32)
        return {'x': x, 'W_res': W_res, 'W_pre': W_pre, 'W_post': W_post, 'H_res_base': H_res_base, 'H_pre_base': H_pre_base, 'H_post_base': H_post_base, 'gate': gate, 'W_branch': W_branch}
    _L0_ffn_all = _L0_ffn_setup()
    _L0_ffn_in = {k: v for k, v in _L0_ffn_all.items() if k in ('W_res', 'W_pre', 'W_post', 'H_res_base', 'H_pre_base', 'H_post_base', 'gate', 'W_branch')}
    del _L0_ffn_all
    return {'x': x, 'itok_B_3_7': itok_B_3_7, 'L0_cond_weight': _L0_cond_in['weight'], 'L0_ffn_W_res': _L0_ffn_in['W_res'], 'L0_ffn_W_pre': _L0_ffn_in['W_pre'], 'L0_ffn_W_post': _L0_ffn_in['W_post'], 'L0_ffn_H_res_base': _L0_ffn_in['H_res_base'], 'L0_ffn_H_pre_base': _L0_ffn_in['H_pre_base'], 'L0_ffn_H_post_base': _L0_ffn_in['H_post_base'], 'L0_ffn_gate': _L0_ffn_in['gate'], 'L0_ffn_W_branch': _L0_ffn_in['W_branch']}

def reference(x, itok_B_3_7, L0_cond_weight, L0_ffn_W_res, L0_ffn_W_pre, L0_ffn_W_post, L0_ffn_H_res_base, L0_ffn_H_pre_base, L0_ffn_H_post_base, L0_ffn_gate, L0_ffn_W_branch):
    import jax
    import jax.numpy as jnp

    def _L0_cond_ref(x, weight, adapter_ids):
        import jax, jax.numpy as jnp
        import numpy as np
        MAX_LORAS, OUT, IN = (8, 2048, 2048)
        B, S = (4, 1024)
        w = weight[adapter_ids]
        return jnp.einsum('bsi,boi->bso', x, w)

    def _L0_ffn_ref(x, W_res, W_pre, W_post, H_res_base, H_pre_base, H_post_base, gate, W_branch):
        import jax, jax.numpy as jnp
        import numpy as np
        N_STREAMS = 4
        DIM = 512
        SINKHORN_ITERS = 50
        SINKHORN_TAU = 0.1
        RMS_EPS = 1.1920929e-07

        def sinkhorn_log(logits, num_iters=SINKHORN_ITERS, tau=SINKHORN_TAU):
            Z = logits / tau
            u0 = jnp.zeros(Z.shape[:-1], Z.dtype)
            v0 = jnp.zeros_like(u0)

            def step(carry, _):
                u, v = carry
                u = -jax.nn.logsumexp(Z + v[..., None, :], axis=-1)
                v = -jax.nn.logsumexp(Z + u[..., :, None], axis=-2)
                return ((u, v), None)
            (u, v), _ = jax.lax.scan(step, (u0, v0), None, length=num_iters)
            return jnp.exp(Z + u[..., :, None] + v[..., None, :])
        B, T, nC = x.shape
        n = N_STREAMS
        C = nC // n
        x_norm = x * jax.lax.rsqrt(jnp.mean(x * x, axis=-1, keepdims=True) + RMS_EPS)
        H_res_logits = (x_norm @ W_res.T).reshape(B, T, n, n) + H_res_base
        H_pre_logits = x_norm @ W_pre.T + H_pre_base
        H_post_logits = x_norm @ W_post.T + H_post_base
        H_res = sinkhorn_log(H_res_logits)
        H_pre = jax.nn.softmax(H_pre_logits, axis=-1)
        H_post = jax.nn.softmax(H_post_logits, axis=-1)
        g = jax.nn.sigmoid(gate)[0]
        I = jnp.eye(n, dtype=H_res.dtype)
        H_res = (1.0 - g) * I + g * H_res
        x_streams = x.reshape(B, T, n, C)
        x_pre = jnp.einsum('btnc,btn->btc', x_streams, H_pre)
        y = x_pre @ W_branch
        x_mixed = jnp.einsum('btij,btjc->btic', H_res, x_streams)
        y_distributed = jnp.einsum('btc,btn->btnc', y, H_post)
        return (x_mixed + y_distributed).reshape(B, T, nC)
    x = x + _L0_ffn_ref(_L0_cond_ref(x, L0_cond_weight, itok_B_3_7), L0_ffn_W_res, L0_ffn_W_pre, L0_ffn_W_post, L0_ffn_H_res_base, L0_ffn_H_pre_base, L0_ffn_H_post_base, L0_ffn_gate, L0_ffn_W_branch)
    return x

_drawn_inputs = setup_inputs


def setup_inputs(seed=0):
    import zlib

    import numpy as np

    out = dict(_drawn_inputs(seed))
    spreads = {'L0_ffn_H_post_base': (0.0, 0.8)}
    factors = {}
    for name, (base, spread) in spreads.items():
        noise = np.random.default_rng([zlib.crc32(name.encode()), seed]).standard_normal(out[name].shape)
        drawn = base * np.exp(spread * noise) if base else spread * noise
        out[name] = jnp.asarray(drawn.astype(out[name].dtype))
    for name, factor in factors.items():
        out[name] = (out[name] * factor).astype(out[name].dtype)
    return out
```

```python
from contextlib import ExitStack

import numpy as np

import concourse.bass as bass
from concourse import mybir

F32 = mybir.dt.float32
F32R = mybir.dt.float32r
I32 = mybir.dt.int32
ACT = mybir.ActivationFunctionType
ALU = mybir.AluOpType
AX = mybir.AxisListType.X

P = 128
BATCHES, TOKENS, DIM = 8, 512, 2048
ADAPTERS = 8
STREAMS = 4
C = DIM // STREAMS
TILES = TOKENS // P
CHUNKS = DIM // P
UNIT_CHUNKS = 2
PASS_UNITS = CHUNKS // UNIT_CHUNKS
UNITS = STREAMS * PASS_UNITS
PAIRS = UNITS // 2
LO_SLOTS = 8
HI_SLOTS = 4
PAIR_SLOTS = LO_SLOTS // 2
NRES = STREAMS * STREAMS
NLOGIT = NRES + 2 * STREAMS
GATE = NLOGIT
MIX_PAIRS = TILES * 2
OUT_SLOTS = 4
RMS_EPS = 1.1920929e-07
TAU = 0.1
BLOCKS = 2
FAST = 24
BLOCK_UNITS = 6
FAST_PER_UNIT = FAST // BLOCK_UNITS

VECTOR_SUBS = (0, 1, 2, 3, 4, 5, 6, 31)
VS = len(VECTOR_SUBS)
GPSIMD_SUBS = tuple(U for U in range(UNITS) if U not in VECTOR_SUBS)
GS = len(GPSIMD_SUBS)

STATS_AT = 5
BLOCK_AT = (5, 12)
FINAL_AT = 19
PRE_AT = (9, 16)
PRE_T_AT = (10, 17, 23, 26)
Y_AT = (11, 18, 24, 27)
MIX_AT = 20
RESIDUAL_AT = 14
STORE_AT = 21
DVE_STEPS = 404
ASKS, DONES = 9, 10
ROWMAX, LOG, SUM, COLMAX, A, B, INV = range(7)


def build(nc, xt, xn, wt, ids, wall, base, wb, out):
    ctx = ExitStack()
    with ctx:
        def sb(name, shape, dt=F32):
            return ctx.enter_context(nc.sbuf_tensor(name, shape, dt))

        def ps(name, shape):
            return ctx.enter_context(nc.psum_tensor(name, shape, F32))

        def sem(name):
            return ctx.enter_context(nc.semaphore(name))

        def raw_and_low(name, shape):
            place = nc.sbuf_base
            raw = sb(name + "_raw", shape)
            assert nc.sbuf_base - place == int(np.prod(shape[1:])) * 4
            return raw, nc.alloc_sbuf_tensor_at(name + "_lo", shape, F32R, offset=place)

        x_hi = sb("x_hi", [P, CHUNKS, TOKENS], F32R)
        x_raw, x_lo = raw_and_low("x", [P, CHUNKS, TOKENS])
        w_raw, w_lo = raw_and_low("w", [P, LO_SLOTS, UNIT_CHUNKS, C])
        w_hi = sb("w_hi", [P, HI_SLOTS, UNIT_CHUNKS, C], F32R)
        cond = sb("cond", [P, 2, STREAMS, TILES, C])
        piece = sb("piece", [P, OUT_SLOTS, 2, C])
        cond_t = sb("cond_t", [P, C])
        xpre = sb("xpre", [P, C])
        wall_sb = sb("wall_sb", [P, CHUNKS, NLOGIT])
        wb_sb = sb("wb_sb", [P, C // P, C])
        ident = sb("ident", [P, P])
        base_sb = sb("base_sb", [P, NLOGIT + 1])
        logit = sb("logit", [P, TILES, NLOGIT])
        kern = sb("kern", [P, TILES * NRES])
        work = sb("work", [P, TILES * NRES])
        vec = sb("vec", [P, 7, TILES * STREAMS])
        ssq = sb("ssq", [P, TILES, STREAMS])
        gate = sb("gate", [P, 3])

        acc = [ps(f"acc{t}", [P, C]) for t in range(TILES)]
        logit_ps = ps("logit_ps", [P, C])
        turn_ps = ps("turn_ps", [P, C])
        y_ps = [ps(f"y_ps{i}", [P, C]) for i in range(2)]

        w_in = [sem(f"w_in{i}") for i in range(PAIR_SLOTS)]
        x_in = [sem(f"x_in{i}") for i in range(PASS_UNITS)]
        const_in = sem("const_in")
        ident_zero, ident_ready = sem("ident_zero"), sem("ident_ready")
        w_hi_ready = sem("w_hi_ready")
        w_lo_vector, w_lo_gpsimd = sem("w_lo_vector"), sem("w_lo_gpsimd")
        x_hi_ready, x_lo_ready = sem("x_hi_ready"), sem("x_lo_ready")
        unit_done = sem("unit_done")
        acc_done = sem("acc_done")
        cond_ready = sem("cond_ready")
        acc_free = sem("acc_free")
        turn_done, cond_t_ready = sem("turn_done"), sem("cond_t_ready")
        project_done = sem("project_done")
        stats_read = sem("stats_read")
        act_ask, act_done = sem("act_ask"), sem("act_done")
        gate_exp, gate_ready = sem("gate_exp"), sem("gate_ready")
        pre_ready, pre_turned, pre_t_ready = sem("pre_ready"), sem("pre_turned"), sem("pre_t_ready")
        y_ready = sem("y_ready")
        step = sem("step")
        mixed = sem("mixed")
        residual_in = [sem(f"residual_in{i}") for i in range(OUT_SLOTS)]
        stored = [sem(f"stored{i}") for i in range(OUT_SLOTS)]

        block = ctx.enter_context(nc.Block())

        def wait_unit(eng, b, unit):
            n, u = divmod(unit, PASS_UNITS)
            if isinstance(b, int) and b * UNITS + unit < 0:
                return
            if u < PASS_UNITS - 1:
                eng.wait_ge(unit_done, (b * STREAMS + n) * (PASS_UNITS - 1) + u + 1)
            else:
                eng.wait_ge(acc_done, (b * STREAMS + n + 1) * TILES)

        def wait_raw_weights(eng, b, unit):
            pair = unit // 2
            eng.wait_ge(w_in[pair % PAIR_SLOTS],
                        (b * (PAIRS // PAIR_SLOTS) + pair // PAIR_SLOTS + 1) * 16)

        def batches(eng, body):
            body(0, 0, True, False)
            with eng.Fori(0, (BATCHES - 2) // 2) as i:
                body(i * 2 + 1, 1, True, True)
                body(i * 2 + 2, 0, True, True)
            body(BATCHES - 1, 1, True, True)
            body(BATCHES, 0, False, True)

        @block.sync
        def _(sp):
            sp.dma_start(base_sb[:], base.to_broadcast([P, NLOGIT + 1])).then_inc(const_in, 16)

            def index(value):
                return value if isinstance(value, int) else sp.snap(value)

            def load_weights(adapter, b, pair):
                slot = pair % PAIR_SLOTS
                place = index(adapter * PAIRS + pair % PAIRS)
                wait_unit(sp, b, 2 * pair - LO_SLOTS + 1)
                sp.dma_start(w_raw[:, 2 * slot:2 * slot + 2, :, :],
                             wt[bass.ds(place, 1), :, :]
                             .rearrange("a p (u k c) -> (a p) u k c", u=2, k=UNIT_CHUNKS)
                             ).then_inc(w_in[slot], 16)

            def load_x(b, u, pieces_of=None):
                place = index(b * PASS_UNITS + u)
                if pieces_of is not None:
                    counts = [index((pieces_of * 2) * 16)] * OUT_SLOTS
                wait_unit(sp, b - 1, 3 * PASS_UNITS + u)
                if pieces_of is not None:
                    for slot in range(OUT_SLOTS):
                        sp.wait_ge(stored[slot], counts[slot])
                sp.dma_start(x_raw[:, 2 * u:2 * u + 2, :],
                             xt[bass.ds(place, 1), :, :]
                             .rearrange("a p (k s) -> (a p) k s", k=UNIT_CHUNKS)
                             ).then_inc(x_in[u], 16)

            def rows(t, place):
                return t[bass.ds(place, 1), :, :].rearrange("a p (s c) -> (a p) s c", s=2)

            def body(b, parity, run, end):
                adapter = None
                if run:
                    adapter = sp.value_load(ids[0:1, bass.ds(b, 1)], min_val=0,
                                            max_val=ADAPTERS - 1)
                    if not end:
                        for u in range(PASS_UNITS):
                            if u < 3:
                                load_weights(adapter, b, u)
                            load_x(b, u)
                            if u == 3:
                                sp.dma_start(wall_sb[:], wall).then_inc(const_in, 16)
                                sp.dma_start(wb_sb[:], wb).then_inc(const_in, 16)
                    else:
                        load_x(b, PASS_UNITS - 1)
                for U in range(UNITS):
                    if run and U % 2 == 0 and U // 2 + 3 < PAIRS:
                        load_weights(adapter, b, U // 2 + 3)
                    last = isinstance(b, int) and b == BATCHES - 1
                    if run and not last:
                        if U == UNITS - 6:
                            following = sp.value_load(ids[0:1, bass.ds(b + 1, 1)], min_val=0,
                                                      max_val=ADAPTERS - 1)
                        if U % 2 == 0 and U // 2 + 3 >= PAIRS:
                            load_weights(following, b, U // 2 + 3)
                        if U > 3 * PASS_UNITS:
                            load_x(b + 1, U - 3 * PASS_UNITS - 1,
                                   pieces_of=b if end and U == UNITS - 1 else None)
                    if end:
                        q = U - RESIDUAL_AT
                        if 0 <= q < OUT_SLOTS:
                            sp.dma_start(piece[:, q, :, :],
                                         rows(xn, index((b - 1) * MIX_PAIRS + q))
                                         ).then_inc(residual_in[q], 16)
                        q = U - STORE_AT
                        if 0 <= q < MIX_PAIRS:
                            place, slot = index((b - 1) * MIX_PAIRS + q), q % OUT_SLOTS
                            sp.wait_ge(mixed, 1 + (b - 1) * MIX_PAIRS + q + 1)
                            sp.dma_start(rows(out, place), piece[:, slot, :, :]
                                         ).then_inc(stored[slot], 16)
                        q = U - STORE_AT - 1
                        if 0 <= q < OUT_SLOTS:
                            place = index((b - 1) * MIX_PAIRS + q + OUT_SLOTS)
                            sp.wait_ge(stored[q], ((b - 1) * 2 + 1) * 16)
                            sp.dma_start(piece[:, q, :, :], rows(xn, place)
                                         ).then_inc(residual_in[q], 16)

            batches(sp, body)
            for slot in range(OUT_SLOTS):
                sp.wait_ge(stored[slot], BATCHES * 2 * 16)

        @block.gpsimd
        def _(pool):
            nc.gpsimd.memset(ident[:], 0.0).then_inc(ident_zero, 1)
            pool.wait_ge(ident_zero, 1)
            nc.gpsimd.affine_select(out=ident[:], in_=ident[:], compare_op=ALU.not_equal,
                                    fill=1.0, base=0, pattern=[[-1, P]],
                                    channel_multiplier=1).then_inc(ident_ready, 1)

            def w_low(b, unit):
                pool.wait_ge(w_hi_ready, b * UNITS + unit + 1)
                lo, hi = unit % LO_SLOTS, unit % HI_SLOTS
                nc.gpsimd.tensor_tensor(w_lo[:, lo, :, :], w_raw[:, lo, :, :],
                                        w_hi[:, hi, :, :].bitcast(F32), ALU.subtract
                                        ).then_inc(w_lo_gpsimd, 1)

            def x_low(b, u):
                pool.wait_ge(x_hi_ready, b * PASS_UNITS + u + 1)
                ks = slice(2 * u, 2 * u + 2)
                nc.gpsimd.tensor_tensor(x_lo[:, ks, :], x_raw[:, ks, :],
                                        x_hi[:, ks, :].bitcast(F32), ALU.subtract
                                        ).then_inc(x_lo_ready, 1)

            def body(b, parity, run, end):
                if not run:
                    return
                if not end:
                    for u in range(PASS_UNITS):
                        x_low(b, u)
                last = isinstance(b, int) and b == BATCHES - 1
                for U in range(UNITS):
                    if end and U < 2:
                        x_low(b, PASS_UNITS - 2 + U)
                    if U + 2 < UNITS and U + 2 not in VECTOR_SUBS:
                        w_low(b, U + 2)
                    if U >= 3 * PASS_UNITS + 2 and not last:
                        x_low(b + 1, U - 3 * PASS_UNITS - 2)

            batches(pool, body)

        @block.scalar
        def _(act):
            def w_high(b, unit):
                wait_raw_weights(act, b, unit)
                wait_unit(act, b, unit - HI_SLOTS)
                nc.scalar.activation(w_hi[:, unit % HI_SLOTS, :, :],
                                     w_raw[:, unit % LO_SLOTS, :, :], ACT.Copy
                                     ).then_inc(w_hi_ready, 1)

            def x_high(b, u):
                act.wait_ge(x_in[u], (b + 1) * 16)
                ks = slice(2 * u, 2 * u + 2)
                nc.scalar.activation(x_hi[:, ks, :], x_raw[:, ks, :], ACT.Copy
                                     ).then_inc(x_hi_ready, 1)

            def evacuate(b, parity, n, t):
                done = (b * STREAMS + n) * TILES + t + 1
                act.wait_ge(acc_done, done)
                if n == 0 and t == 0 and not (isinstance(b, int) and b == 0):
                    act.wait_ge(stats_read, b)
                if n == 0 and not (isinstance(b, int) and b < 2):
                    act.wait_ge(mixed, 1 + (b - 1) * MIX_PAIRS)
                nc.scalar.activation(cond[:, parity, n, t, :], acc[t][:], ACT.Copy
                                     ).then_inc(cond_ready, 1)
                act.wait_ge(cond_ready, done)
                nc.scalar.activation(acc[t][:], acc[t][:], ACT.Square,
                                     accum_out=ssq[:, t, n:n + 1]).then_inc(acc_free, 1)

            def tile_of_previous_pass(b, parity, n, t):
                if n > 0:
                    evacuate(b, parity, n - 1, t)
                else:
                    evacuate(b - 1, 1 - parity, STREAMS - 1, t)

            def evacuate_turned(job):
                act.wait_ge(turn_done, job + 1)
                if not (isinstance(job, int) and job == 0):
                    act.wait_ge(project_done, job)
                nc.scalar.activation(cond_t[:], turn_ps[:], ACT.Copy).then_inc(cond_t_ready, 1)

            def answer(asked, o, i, func, scale=1.0):
                act.wait_ge(act_ask, asked)
                nc.scalar.activation(o, i, func, scale=scale).then_inc(act_done, 1)

            def body(b, parity, run, end):
                last = isinstance(b, int) and b == BATCHES - 1
                if run and not end:
                    act.wait_ge(const_in, 48)
                    nc.scalar.activation(gate[:, 0:1], base_sb[:, GATE:GATE + 1], ACT.Exp,
                                         scale=-1.0).then_inc(gate_exp, 1)
                    for u in range(PASS_UNITS):
                        x_high(b, u)
                        if u < 3:
                            w_high(b, u)
                asks, dones = (b - 1) * ASKS, (b - 1) * DONES
                for U in range(UNITS):
                    n, u = divmod(U, PASS_UNITS)
                    if u == 0 and (n > 0 and run or n == 0 and end):
                        tile_of_previous_pass(b, parity, n, TILES - 1)
                    if 1 <= u <= TILES and (n > 0 and run or n == 0 and end):
                        evacuate_turned((b * STREAMS + n - 1) * TILES + u - 1)
                    if end and run and U < 2:
                        x_high(b, PASS_UNITS - 2 + U)
                    if run and U + HI_SLOTS - 1 < UNITS:
                        w_high(b, U + HI_SLOTS - 1)
                    elif run and not last:
                        w_high(b + 1, U + HI_SLOTS - 1 - UNITS)
                    if run and not last and U >= 3 * PASS_UNITS + 2:
                        x_high(b + 1, U - 3 * PASS_UNITS - 2)
                    if end and U == STATS_AT:
                        answer(asks + 1, vec[:, 1, 0:TILES], vec[:, 0, 0:TILES], ACT.Ln)
                        act.wait_ge(act_done, dones + 1)
                        nc.scalar.activation(vec[:, 2, 0:TILES], vec[:, 1, 0:TILES], ACT.Exp,
                                             scale=-0.5).then_inc(act_done, 1)
                        heads = logit[:, :, NRES:NLOGIT]
                        answer(asks + 2, heads, heads, ACT.Exp)
                    if end and U in BLOCK_AT:
                        ask = asks + (3 if U == BLOCK_AT[0] else 6)
                        if U == BLOCK_AT[1]:
                            answer(ask, vec[:, LOG, :], vec[:, SUM, :], ACT.Ln)
                            ask = ask + 1
                        answer(ask, work[:], work[:], ACT.Exp)
                        answer(ask + 1, vec[:, LOG, :], vec[:, SUM, :], ACT.Ln)
                        answer(ask + 2, work[:], work[:], ACT.Exp)
                    for t in range(TILES):
                        if end and U == PRE_T_AT[t] + 1:
                            act.wait_ge(pre_turned, (b - 1) * TILES + t + 1)
                            nc.scalar.activation(xpre[:], y_ps[t % 2][:], ACT.Copy
                                                 ).then_inc(pre_t_ready, 1)
                    if run and u == PASS_UNITS - 1:
                        for t in range(TILES - 1):
                            evacuate(b, parity, n, t)

            batches(act, body)

        @block.vector
        def _(dve):
            def w_low(b, unit):
                dve.wait_ge(w_hi_ready, b * UNITS + unit + 1)
                lo, hi = unit % LO_SLOTS, unit % HI_SLOTS
                nc.vector.tensor_tensor(w_lo[:, lo, :, :], w_raw[:, lo, :, :],
                                        w_hi[:, hi, :, :].bitcast(F32), ALU.subtract
                                        ).then_inc(w_lo_vector, 1)

            def body(b, parity, run, end):
                first = not end
                last = isinstance(b, int) and b == BATCHES - 1
                c = b - 1
                count = [0]

                def mark(ins):
                    ins.then_inc(step, 1)
                    count[0] += 1
                    return count[0]

                def after(number):
                    dve.wait_ge(step, c * DVE_STEPS + number)

                def link(ins):
                    after(mark(ins))

                asked = [0, 0]

                def ask(ins, dones=1):
                    ins.then_inc(act_ask, 1)
                    asked[1] += dones
                    dve.wait_ge(act_done, c * DONES + asked[1])

                tt, reduce = nc.vector.tensor_tensor, nc.vector.tensor_reduce
                by_row = "p (t i j) -> p t i j"
                work_r = work[:].rearrange(by_row, i=STREAMS, j=STREAMS)
                work_c = work[:].rearrange("p (t i j) -> p t j i", i=STREAMS, j=STREAMS)
                kern_r = kern[:].rearrange(by_row, i=STREAMS, j=STREAMS)
                kern_c = kern[:].rearrange("p (t i j) -> p t j i", i=STREAMS, j=STREAMS)
                z_r = logit[:, :, 0:NRES].rearrange("p t (i j) -> p t i j", j=STREAMS)

                def small(k):
                    return vec[:, k, :].rearrange("p (t i) -> p t i", i=STREAMS)

                def over_rows(k):
                    return small(k).unsqueeze(3).to_broadcast([P, TILES, STREAMS, STREAMS])

                def over_columns(k):
                    return small(k).unsqueeze(2).to_broadcast([P, TILES, STREAMS, STREAMS])

                def statistics():
                    dve.wait_ge(acc_free, b * STREAMS * TILES)
                    link(reduce(vec[:, 0, 0:TILES], ssq[:], AX, ALU.add))
                    ask(nc.vector.tensor_scalar(vec[:, 0, 0:TILES], vec[:, 0, 0:TILES], 1.0 / DIM,
                                                RMS_EPS, ALU.mult, ALU.add), dones=2)
                    ms, r0, t = vec[:, 0, 0:TILES], vec[:, 2, 0:TILES], vec[:, 4, 0:TILES]
                    link(tt(t, r0, r0, ALU.mult))
                    link(tt(t, t, ms, ALU.mult))
                    link(nc.vector.tensor_scalar(t, t, -0.5, 1.5, ALU.mult, ALU.add))
                    link(tt(vec[:, 5, 0:TILES], r0, t, ALU.mult))
                    dve.wait_ge(project_done, b * STREAMS * TILES)
                    tt(logit[:], logit_ps[:, 0:TILES * NLOGIT].rearrange(
                        "p (t l) -> p t l", l=NLOGIT),
                       vec[:, 5, 0:TILES].unsqueeze(2).to_broadcast([P, TILES, NLOGIT]),
                       ALU.mult).then_inc(stats_read, 1)
                    dve.wait_ge(stats_read, b)
                    link(tt(logit[:], logit[:],
                            base_sb[:, 0:NLOGIT].unsqueeze(1).to_broadcast([P, TILES, NLOGIT]),
                            ALU.add))
                    heads = logit[:, :, NRES:NLOGIT].rearrange("p t (h j) -> p t h j", j=STREAMS)
                    eight = vec[:, 0:2, :].rearrange("p k f -> p (k f)")[:, 0:2 * TILES]
                    head = eight.rearrange("p (t h) -> p t h", h=2)
                    head_b = head.unsqueeze(3).to_broadcast([P, TILES, 2, STREAMS])
                    link(reduce(head, heads, AX, ALU.max))
                    ask(tt(heads, heads, head_b, ALU.subtract))
                    link(reduce(head, heads, AX, ALU.add))
                    link(nc.vector.reciprocal(eight, eight))
                    link(tt(heads, heads, head_b, ALU.mult))
                    z = logit[:, :, 0:NRES]
                    link(nc.vector.tensor_scalar(z, z, 1.0 / TAU, None, ALU.mult))

                def log_step(k):
                    if k == 0:
                        source = z_r
                    else:
                        ask(tt(vec[:, SUM, :], vec[:, B, :], vec[:, INV, :], ALU.mult))
                        link(tt(vec[:, COLMAX, :], vec[:, LOG, :], vec[:, COLMAX, :],
                                ALU.subtract))
                        link(tt(work_r, z_r, over_columns(COLMAX), ALU.add))
                        source = work_r
                    link(reduce(small(ROWMAX), source, AX, ALU.max))
                    ask(tt(work_r, source, over_rows(ROWMAX), ALU.subtract))
                    ask(reduce(small(SUM), work_r, AX, ALU.add))
                    link(tt(vec[:, ROWMAX, :], vec[:, ROWMAX, :], vec[:, LOG, :], ALU.add))
                    link(tt(work_r, z_r, over_rows(ROWMAX), ALU.subtract))
                    link(reduce(small(COLMAX), work_c, AX, ALU.max))
                    ask(tt(work_r, work_r, over_columns(COLMAX), ALU.subtract))
                    link(reduce(small(INV), work_c, AX, ALU.add))
                    link(nc.vector.reciprocal(vec[:, INV, :], vec[:, INV, :]))
                    link(tt(kern_r, work_r, over_columns(INV), ALU.mult))
                    link(tt(work_r, work_r, over_columns(INV), ALU.mult))

                def fast_step():
                    link(reduce(small(A), work_r, AX, ALU.add))
                    link(nc.vector.reciprocal(vec[:, A, :], vec[:, A, :]))
                    link(tt(work_r, kern_r, over_rows(A), ALU.mult))
                    link(reduce(small(B), work_c, AX, ALU.add))
                    link(nc.vector.reciprocal(vec[:, B, :], vec[:, B, :]))
                    link(tt(work_r, kern_r, over_columns(B), ALU.mult))

                def final_matrix():
                    link(tt(kern_r, work_r, over_rows(A), ALU.mult))
                    link(nc.vector.tensor_scalar(kern[:], kern[:], gate[:, 1:2], None, ALU.mult))
                    diagonal = kern[:].rearrange("p (t f) -> p t f", f=NRES)[
                        :, :, 0:NRES:STREAMS + 1]
                    link(nc.vector.tensor_scalar(diagonal, diagonal, gate[:, 2:3], None, ALU.add))

                def pre(t):
                    if t > 0:
                        dve.wait_ge(y_ready, c * TILES + t)
                    for j in range(STREAMS):
                        weight = logit[:, t, NRES + j:NRES + j + 1]
                        source = cond[:, 1 - parity, j, t, :]
                        if j == 0:
                            link(nc.vector.tensor_scalar(xpre[:], source, weight, None, ALU.mult))
                            continue
                        ins = nc.vector.scalar_tensor_tensor(
                            out=xpre[:], in0=source, scalar=weight, in1=xpre[:],
                            op0=ALU.mult, op1=ALU.add)
                        if j < STREAMS - 1:
                            link(ins)
                        else:
                            ins.then_inc(pre_ready, 1)

                def mix(t, p):
                    q = 2 * t + p
                    slot = q % OUT_SLOTS
                    dve.wait_ge(residual_in[slot], (c * 2 + q // OUT_SLOTS + 1) * 16)
                    written = [0, 0]
                    for j in range(STREAMS + 1):
                        for s in range(2):
                            i = 2 * p + s
                            if j < STREAMS:
                                source = cond[:, 1 - parity, j, t, :]
                                weight = kern[:, t * NRES + i * STREAMS + j:][:, 0:1]
                            else:
                                source = y_ps[t % 2][:]
                                weight = logit[:, t, NRES + STREAMS + i:][:, 0:1]
                                if s == 0:
                                    dve.wait_ge(y_ready, c * TILES + t + 1)
                            if j > 0:
                                after(written[s])
                            ins = nc.vector.scalar_tensor_tensor(
                                out=piece[:, slot, s, :], in0=source, scalar=weight,
                                in1=piece[:, slot, s, :], op0=ALU.mult, op1=ALU.add)
                            if j == STREAMS and s == 1:
                                ins.then_inc(mixed, 1)
                            else:
                                written[s] = mark(ins)

                if first:
                    dve.wait_ge(gate_exp, 1)
                    g = nc.vector.tensor_scalar(gate[:, 1:2], gate[:, 0:1], 1.0, None, ALU.add)
                    g.then_inc(gate_ready, 1)
                    dve.wait_ge(gate_ready, 1)
                    nc.vector.reciprocal(gate[:, 1:2], gate[:, 1:2]).then_inc(gate_ready, 1)
                    dve.wait_ge(gate_ready, 2)
                    nc.vector.tensor_scalar(gate[:, 2:3], gate[:, 1:2], -1.0, 1.0, ALU.mult,
                                            ALU.add).then_inc(mixed, 1)
                    dve.wait_ge(mixed, 1)
                    w_low(b, 0)
                    w_low(b, 1)
                for U in range(UNITS):
                    if run and U + 2 in VECTOR_SUBS:
                        w_low(b, U + 2)
                    if run and not last and U + 2 >= UNITS:
                        w_low(b + 1, U + 2 - UNITS)
                    if not end:
                        continue
                    if U == STATS_AT:
                        statistics()
                    for k in range(BLOCKS):
                        if U == BLOCK_AT[k]:
                            log_step(k)
                    for t in range(len(PRE_AT)):
                        if U == PRE_AT[t]:
                            pre(t)
                    if any(at < U <= at + BLOCK_UNITS for at in BLOCK_AT):
                        for _ in range(FAST_PER_UNIT):
                            fast_step()
                    if U == FINAL_AT:
                        final_matrix()
                    q = U - MIX_AT
                    if q in (2, 4):
                        pre(q // 2 + 1)
                    if 0 <= q < MIX_PAIRS:
                        mix(q // 2, q % 2)
                if end:
                    assert count[0] == DVE_STEPS, count[0]

            batches(dve, body)

        @block.tensor
        def _(pe):
            def unit(b, U):
                n, u = divmod(U, PASS_UNITS)
                if U in VECTOR_SUBS:
                    pe.wait_ge(w_lo_vector, b * VS + VECTOR_SUBS.index(U) + 1)
                else:
                    pe.wait_ge(w_lo_gpsimd, b * GS + GPSIMD_SUBS.index(U) + 1)
                if n == 0:
                    pe.wait_ge(x_lo_ready, b * PASS_UNITS + u + 1)
                for t in range(TILES):
                    if u == 0 and not (n == 0 and isinstance(b, int) and b == 0):
                        pe.wait_ge(acc_free, (b * STREAMS + n - 1) * TILES + t + 1)
                    rows = slice(t * P, (t + 1) * P)
                    for k in range(UNIT_CHUNKS):
                        chunk = UNIT_CHUNKS * u + k
                        wh, wl = w_hi[:, U % HI_SLOTS, k, :], w_lo[:, U % LO_SLOTS, k, :]
                        xh, xl = x_hi[:, chunk, rows], x_lo[:, chunk, rows]
                        for m, (stationary, moving) in enumerate(((xh, wh), (xh, wl), (xl, wh))):
                            mm = nc.tensor.matmul(acc[t][:], stationary, moving,
                                                  start=(chunk == 0 and m == 0),
                                                  stop=(chunk == CHUNKS - 1 and m == 2))
                    if u == PASS_UNITS - 1:
                        mm.then_inc(acc_done, 1)
                if u < PASS_UNITS - 1:
                    mm.then_inc(unit_done, 1)

            def turn(source, job):
                pe.wait_ge(cond_ready, job + 1)
                if not (isinstance(job, int) and job == 0):
                    pe.wait_ge(cond_t_ready, job)
                for k in range(C // P):
                    mm = nc.tensor.transpose(turn_ps[:, k * P:(k + 1) * P],
                                             source[:, k * P:(k + 1) * P], ident[:])
                mm.then_inc(turn_done, 1)

            def project(n, t, job):
                pe.wait_ge(cond_t_ready, job + 1)
                for k in range(C // P):
                    mm = nc.tensor.matmul(logit_ps[:, t * NLOGIT:(t + 1) * NLOGIT],
                                          cond_t[:, k * P:(k + 1) * P],
                                          wall_sb[:, n * (C // P) + k, :],
                                          start=(n == 0 and t == 0 and k == 0),
                                          stop=(n == STREAMS - 1 and k == C // P - 1),
                                          skip_group_check=True)
                mm.then_inc(project_done, 1)

            def body(b, parity, run, end):
                if run and not end:
                    pe.wait_ge(ident_ready, 1)
                    pe.wait_ge(const_in, 48)
                c = b - 1
                for U in range(UNITS):
                    n, u = divmod(U, PASS_UNITS)
                    if run:
                        unit(b, U)
                    if n > 0 and run or n == 0 and end:
                        job = (b * STREAMS + n - 1) * TILES
                        plane, side = (n - 1, parity) if n > 0 else (STREAMS - 1, 1 - parity)
                        if 1 <= u <= TILES:
                            if n == 1 and u == 1 and not (isinstance(b, int) and b == 0):
                                pe.wait_ge(stats_read, b)
                            project(plane, u - 1, job + u - 1)
                        if u < TILES:
                            turn(cond[:, side, plane, u, :], job + u)
                    for t in range(TILES):
                        tile = c * TILES + t
                        bank = y_ps[t % 2]
                        if end and U == PRE_T_AT[t]:
                            pe.wait_ge(pre_ready, tile + 1)
                            pe.wait_ge(mixed, 1 + c * MIX_PAIRS + max(0, t - 1) * 2)
                            for k in range(C // P):
                                cols = slice(k * P, (k + 1) * P)
                                mm = nc.tensor.transpose(bank[:, cols], xpre[:, cols], ident[:])
                            mm.then_inc(pre_turned, 1)
                        if end and U == Y_AT[t]:
                            pe.wait_ge(pre_t_ready, tile + 1)
                            for k in range(C // P):
                                mm = nc.tensor.matmul(bank[:], xpre[:, k * P:(k + 1) * P],
                                                      wb_sb[:, k, :], start=(k == 0),
                                                      stop=(k == C // P - 1))
                            mm.then_inc(y_ready, 1)

            batches(pe, body)


def kernel(x, itok_B_3_7, L0_cond_weight, L0_ffn_W_res, L0_ffn_W_pre, L0_ffn_W_post,
           L0_ffn_H_res_base, L0_ffn_H_pre_base, L0_ffn_H_post_base, L0_ffn_gate, L0_ffn_W_branch):
    import concourse.bacc as bacc
    from concourse.bass_utils import run_bass_kernel_spmd

    x = np.asarray(x)
    weight = np.asarray(L0_cond_weight)
    xt = x.reshape(BATCHES, TOKENS, PASS_UNITS, UNIT_CHUNKS, P).transpose(0, 2, 4, 3, 1)
    wt = weight.reshape(ADAPTERS, STREAMS, C, PASS_UNITS // 2, 2, UNIT_CHUNKS, P)
    wt = wt.transpose(0, 1, 3, 6, 4, 5, 2)
    xn = x.reshape(BATCHES, TILES, P, 2, 2 * C).transpose(0, 1, 3, 2, 4)
    wall = np.concatenate([np.asarray(w) for w in (L0_ffn_W_res, L0_ffn_W_pre, L0_ffn_W_post)])
    base = np.concatenate([np.asarray(v).reshape(-1) for v in (
        L0_ffn_H_res_base, L0_ffn_H_pre_base, L0_ffn_H_post_base, L0_ffn_gate)])
    arrays = {
        "xt": xt.reshape(BATCHES * PASS_UNITS, P, UNIT_CHUNKS * TOKENS),
        "xn": xn.reshape(BATCHES * MIX_PAIRS, P, 2 * C),
        "wt": wt.reshape(ADAPTERS * PAIRS, P, 2 * UNIT_CHUNKS * C),
        "ids": np.asarray(itok_B_3_7).reshape(1, BATCHES),
        "wall": wall.reshape(NLOGIT, CHUNKS, P).transpose(2, 1, 0),
        "base": base.reshape(1, NLOGIT + 1),
        "wb": np.asarray(L0_ffn_W_branch).reshape(C // P, P, C).transpose(1, 0, 2),
    }
    arrays = {name: np.ascontiguousarray(a) for name, a in arrays.items()}
    nc = bacc.Bacc("TRN2", target_bir_lowering=False, num_devices=1)
    args = [nc.dram_tensor(name, a.shape, mybir.dt.from_np(a.dtype), kind="ExternalInput").ap()
            for name, a in arrays.items()]
    out = nc.dram_tensor("out", (BATCHES * MIX_PAIRS, P, 2 * C), F32, kind="ExternalOutput").ap()
    build(nc, *args, out)
    got = run_bass_kernel_spmd(nc, [arrays], core_ids=[0]).results[0]["out"]
    got = got.reshape(BATCHES, TILES, 2, P, 2 * C).transpose(0, 1, 3, 2, 4)
    return np.ascontiguousarray(got.reshape(BATCHES, TOKENS, DIM))
```

```python
from contextlib import ExitStack

import numpy as np

import concourse.bass as bass
from concourse import mybir

F32 = mybir.dt.float32
F32R = mybir.dt.float32r
I32 = mybir.dt.int32
ACT = mybir.ActivationFunctionType
ALU = mybir.AluOpType
AX = mybir.AxisListType.X

P = 128
BATCHES, TOKENS, DIM = 8, 512, 2048
ADAPTERS = 8
STREAMS = 4
C = DIM // STREAMS
TILES = TOKENS // P
CHUNKS = DIM // P
UNIT_CHUNKS = 2
PASS_UNITS = CHUNKS // UNIT_CHUNKS
UNITS = STREAMS * PASS_UNITS
LO_SLOTS = 4
HI_SLOTS = 4
AHEAD = 2
NRES = STREAMS * STREAMS
NLOGIT = NRES + 2 * STREAMS
GATE = NLOGIT
MIX_PAIRS = TILES * 2
OUT_SLOTS = 4
RMS_EPS = 1.1920929e-07
TAU = 0.1
BLOCKS = 2
FAST = 24

VECTOR_SUBS = (0, 1, 2, 3)
GPSIMD_SUBS = tuple(U for U in range(UNITS) if U not in VECTOR_SUBS)
VS, GS = len(VECTOR_SUBS), len(GPSIMD_SUBS)

TURN_AT = {True: (0, 1, 2, 3), False: (1, 5, 9, 13)}
PROJECT_AT = {True: (1, 2, 3, 4), False: (4, 8, 12, 15)}
SPLIT_AT = {True: (0, 0, 1, 1), False: (1, 3, 5, 7)}
GATHER_AT = 6

STATS_AT = 3
BLOCK_AT = (3, 12)
FAST_AT = ((5, 12), (13, 20))
FINAL_AT = 20
PRE_AT = (8, 15, 21, 23)
PRE_T_AT = (10, 17, 23, 26)
PRE_SPLIT_AT = (11, 18, 24, 27)
Y_AT = (13, 20, 25, 28)
MIX_AT = (21, 22, 23, 24, 26, 27, 28, 29)
RESIDUAL_AT = (14, 15, 16, 17, 24, 25, 26, 27)
STORE_AT = (23, 24, 25, 26, 28, 29, 30, 31)
DVE_STEPS = 404
ASKS, DONES = 9, 10
ROWMAX, LOG, SUM, COLMAX, A, B, INV = range(7)


def build(nc, xt, xn, wt, ids, wall, base, wb, out):
    ctx = ExitStack()
    with ctx:
        def sb(name, shape, dt=F32):
            return ctx.enter_context(nc.sbuf_tensor(name, shape, dt))

        def ps(name, shape):
            return ctx.enter_context(nc.psum_tensor(name, shape, F32))

        def sem(name):
            return ctx.enter_context(nc.semaphore(name))

        def raw_and_low(name, shape):
            place = nc.sbuf_base
            raw = sb(name + "_raw", shape)
            assert nc.sbuf_base - place == int(np.prod(shape[1:])) * 4
            return raw, nc.alloc_sbuf_tensor_at(name + "_lo", shape, F32R, offset=place)

        x_hi = sb("x_hi", [P, CHUNKS, TOKENS], F32R)
        x_raw, x_lo = raw_and_low("x", [P, CHUNKS, TOKENS])
        w_raw, w_lo = raw_and_low("w", [P, LO_SLOTS, UNIT_CHUNKS, C])
        w_hi = sb("w_hi", [P, HI_SLOTS, UNIT_CHUNKS, C], F32R)
        cond = sb("cond", [P, 2, STREAMS, TILES, C])
        piece = sb("piece", [P, OUT_SLOTS, 2, C])
        cond_t = sb("cond_t", [P, 2, TOKENS], F32R)
        xpre = sb("xpre", [P, C])
        xpre_t = sb("xpre_t", [P, 2, C], F32R)
        wall_sb = sb("wall_sb", [P, CHUNKS, 2 * NLOGIT], F32R)
        wb_sb = sb("wb_sb", [P, 2, C // P, C], F32R)
        wall_raw = cond[:, 1, 0, :, :].rearrange("p t c -> p (t c)")[:, 0:CHUNKS * NLOGIT]
        wall_raw = wall_raw.rearrange("p (k l) -> p k l", l=NLOGIT)
        wb_raw = cond[:, 1, 1, :, :]
        ident = sb("ident", [P, P])
        pair_sum = sb("pair_sum", [2 * NLOGIT, NLOGIT])
        base_sb = sb("base_sb", [P, NLOGIT + 1])
        logit = sb("logit", [P, TILES, NLOGIT])
        kern = sb("kern", [P, TILES * NRES])
        work = sb("work", [P, TILES * NRES])
        vec = sb("vec", [P, 7, TILES * STREAMS])
        ssq = sb("ssq", [P, TILES, STREAMS])
        gate = sb("gate", [P, 3])

        acc = [ps(f"acc{t}", [P, C]) for t in range(TILES)]
        logit_ps = ps("logit_ps", [P, C])
        turn_ps = ps("turn_ps", [P, C])
        y_ps = [ps(f"y_ps{i}", [P, C]) for i in range(2)]

        w_in = [sem(f"w_in{i}") for i in range(LO_SLOTS)]
        x_in = [sem(f"x_in{i}") for i in range(PASS_UNITS)]
        base_in, wall_in, wb_in = sem("base_in"), sem("wall_in"), sem("wb_in")
        const_hi, const_ready = sem("const_hi"), sem("const_ready")
        ident_zero, ident_ready = sem("ident_zero"), sem("ident_ready")
        w_hi_ready = sem("w_hi_ready")
        w_lo_vector, w_lo_gpsimd = sem("w_lo_vector"), sem("w_lo_gpsimd")
        x_hi_ready, x_lo_ready = sem("x_hi_ready"), sem("x_lo_ready")
        unit_done = sem("unit_done")
        acc_done = sem("acc_done")
        cond_ready = sem("cond_ready")
        acc_free = sem("acc_free")
        turn_done = sem("turn_done")
        cond_hi_ready, cond_lo_ready = sem("cond_hi_ready"), sem("cond_lo_ready")
        project_done = sem("project_done")
        logit_copied, logit_gathered = sem("logit_copied"), sem("logit_gathered")
        stats_read = sem("stats_read")
        act_ask, act_done = sem("act_ask"), sem("act_done")
        gate_exp, gate_ready = sem("gate_exp"), sem("gate_ready")
        pre_ready, pre_turned = sem("pre_ready"), sem("pre_turned")
        pre_hi_ready, pre_lo_ready = sem("pre_hi_ready"), sem("pre_lo_ready")
        y_ready = sem("y_ready")
        step = sem("step")
        mixed = sem("mixed")
        residual_in = [sem(f"residual_in{i}") for i in range(OUT_SLOTS)]
        stored = [sem(f"stored{i}") for i in range(OUT_SLOTS)]

        block = ctx.enter_context(nc.Block())

        def wait_unit(eng, b, unit):
            n, u = divmod(unit, PASS_UNITS)
            if isinstance(b, int) and b * UNITS + unit < 0:
                return
            if u < PASS_UNITS - 1:
                eng.wait_ge(unit_done, (b * STREAMS + n) * (PASS_UNITS - 1) + u + 1)
            else:
                eng.wait_ge(acc_done, (b * STREAMS + n + 1) * TILES)

        def turned_jobs(plan, n, at):
            return [k for k, when in enumerate(plan[n == 0]) if when == at]

        def batches(eng, body):
            body(0, 0, True, False)
            with eng.Fori(0, (BATCHES - 2) // 2) as i:
                body(i * 2 + 1, 1, True, True)
                body(i * 2 + 2, 0, True, True)
            body(BATCHES - 1, 1, True, True)
            body(BATCHES, 0, False, True)

        @block.sync
        def _(sp):
            def index(value):
                return value if isinstance(value, int) else sp.snap(value)

            def adapter_of(b):
                return sp.value_load(ids[0:1, bass.ds(b, 1)], min_val=0, max_val=ADAPTERS - 1)

            def load_weights(adapter, b, unit):
                slot = unit % LO_SLOTS
                place = index(adapter * UNITS + unit % UNITS)
                wait_unit(sp, b, unit - LO_SLOTS)
                sp.dma_start(w_raw[:, slot, :, :],
                             wt[bass.ds(place, 1), :, :]
                             .rearrange("a p (k c) -> (a p) k c", k=UNIT_CHUNKS)
                             ).then_inc(w_in[slot], 16)

            def load_x(b, u, pieces_of=None):
                place = index(b * PASS_UNITS + u)
                if pieces_of is not None:
                    count = index(pieces_of * 2 * 16)
                wait_unit(sp, b - 1, 3 * PASS_UNITS + u)
                if pieces_of is not None:
                    for slot in range(OUT_SLOTS):
                        sp.wait_ge(stored[slot], count)
                sp.dma_start(x_raw[:, 2 * u:2 * u + 2, :],
                             xt[bass.ds(place, 1), :, :]
                             .rearrange("a p (k s) -> (a p) k s", k=UNIT_CHUNKS)
                             ).then_inc(x_in[u], 16)

            def rows(t, place):
                return t[bass.ds(place, 1), :, :].rearrange("a p (s c) -> (a p) s c", s=2)

            def body(b, parity, run, end):
                last = isinstance(b, int) and b == BATCHES - 1
                if run:
                    adapter = adapter_of(b)
                    if not end:
                        for u in range(PASS_UNITS):
                            load_x(b, u)
                            if u < AHEAD + 1:
                                load_weights(adapter, b, u)
                            if u == 0:
                                sp.dma_start(base_sb[:], base.to_broadcast([P, NLOGIT + 1])
                                             ).then_inc(base_in, 16)
                        sp.dma_start(wall_raw, wall).then_inc(wall_in, 16)
                        sp.dma_start(wb_raw, wb).then_inc(wb_in, 16)
                    else:
                        load_x(b, PASS_UNITS - 1)
                for U in range(UNITS):
                    unit = U + AHEAD + 1
                    if run and unit < UNITS:
                        load_weights(adapter, b, unit)
                    if run and not last:
                        if unit == UNITS - 1:
                            following = adapter_of(b + 1)
                        if unit >= UNITS:
                            load_weights(following, b, unit)
                    for q in range(MIX_PAIRS):
                        slot, use = q % OUT_SLOTS, q // OUT_SLOTS
                        if end and U == STORE_AT[q]:
                            place = index((b - 1) * MIX_PAIRS + q)
                            sp.wait_ge(mixed, 1 + (b - 1) * MIX_PAIRS + q + 1)
                            sp.dma_start(rows(out, place), piece[:, slot, :, :]
                                         ).then_inc(stored[slot], 16)
                        if end and U == RESIDUAL_AT[q]:
                            place = index((b - 1) * MIX_PAIRS + q)
                            if use > 0:
                                sp.wait_ge(stored[slot], ((b - 1) * 2 + 1) * 16)
                            sp.dma_start(piece[:, slot, :, :], rows(xn, place)
                                         ).then_inc(residual_in[slot], 16)
                    if run and not last and U > 3 * PASS_UNITS:
                        load_x(b + 1, U - 3 * PASS_UNITS - 1,
                               pieces_of=b if end and U == UNITS - 1 else None)

            batches(sp, body)
            for slot in range(OUT_SLOTS):
                sp.wait_ge(stored[slot], BATCHES * 2 * 16)

        @block.gpsimd
        def _(pool):
            nc.gpsimd.memset(ident[:], 0.0).then_inc(ident_zero, 1)
            pool.wait_ge(ident_zero, 1)
            nc.gpsimd.affine_select(out=ident[:], in_=ident[:], compare_op=ALU.not_equal,
                                    fill=1.0, base=0, pattern=[[-1, P]],
                                    channel_multiplier=1).then_inc(ident_ready, 1)

            def w_low(b, unit):
                pool.wait_ge(w_hi_ready, b * UNITS + unit + 1)
                lo, hi = unit % LO_SLOTS, unit % HI_SLOTS
                nc.gpsimd.tensor_tensor(w_lo[:, lo, :, :], w_raw[:, lo, :, :],
                                        w_hi[:, hi, :, :].bitcast(F32), ALU.subtract
                                        ).then_inc(w_lo_gpsimd, 1)

            def x_low(b, u):
                pool.wait_ge(x_hi_ready, b * PASS_UNITS + u + 1)
                ks = slice(2 * u, 2 * u + 2)
                nc.gpsimd.tensor_tensor(x_lo[:, ks, :], x_raw[:, ks, :],
                                        x_hi[:, ks, :].bitcast(F32), ALU.subtract
                                        ).then_inc(x_lo_ready, 1)

            def body(b, parity, run, end):
                last = isinstance(b, int) and b == BATCHES - 1
                for U in range(UNITS if run else 0):
                    if U + AHEAD in GPSIMD_SUBS:
                        w_low(b, U + AHEAD)
                    if end and U < 2:
                        x_low(b, PASS_UNITS - 2 + U)
                    if U >= 3 * PASS_UNITS + 2 and not last:
                        x_low(b + 1, U - 3 * PASS_UNITS - 2)

            batches(pool, body)

        @block.scalar
        def _(act):
            def w_high(b, unit):
                act.wait_ge(w_in[unit % LO_SLOTS],
                            (b * (UNITS // LO_SLOTS) + unit // LO_SLOTS + 1) * 16)
                wait_unit(act, b, unit - HI_SLOTS)
                nc.scalar.activation(w_hi[:, unit % HI_SLOTS, :, :],
                                     w_raw[:, unit % LO_SLOTS, :, :], ACT.Copy
                                     ).then_inc(w_hi_ready, 1)

            def x_high(b, u):
                act.wait_ge(x_in[u], (b + 1) * 16)
                ks = slice(2 * u, 2 * u + 2)
                nc.scalar.activation(x_hi[:, ks, :], x_raw[:, ks, :], ACT.Copy
                                     ).then_inc(x_hi_ready, 1)

            def evacuate(b, parity, n, t):
                done = (b * STREAMS + n) * TILES + t + 1
                act.wait_ge(acc_done, done)
                if n == 0 and t == 0 and not (isinstance(b, int) and b == 0):
                    act.wait_ge(stats_read, b)
                if n == 0 and not (isinstance(b, int) and b < 2):
                    act.wait_ge(mixed, 1 + (b - 1) * MIX_PAIRS)
                nc.scalar.activation(cond[:, parity, n, t, :], acc[t][:], ACT.Copy
                                     ).then_inc(cond_ready, 1)
                act.wait_ge(cond_ready, done)
                nc.scalar.activation(acc[t][:], acc[t][:], ACT.Square,
                                     accum_out=ssq[:, t, n:n + 1]).then_inc(acc_free, 1)

            def tile_of_previous_pass(b, parity, n, t):
                if n > 0:
                    evacuate(b, parity, n - 1, t)
                else:
                    evacuate(b - 1, 1 - parity, STREAMS - 1, t)

            def split_turned(job):
                act.wait_ge(turn_done, job + 1)
                if not (isinstance(job, int) and job == 0):
                    act.wait_ge(project_done, job)
                nc.scalar.activation(cond_t[:, 0, :], turn_ps[:], ACT.Copy
                                     ).then_inc(cond_hi_ready, 1)

            def answer(asked, o, i, func, scale=1.0):
                act.wait_ge(act_ask, asked)
                nc.scalar.activation(o, i, func, scale=scale).then_inc(act_done, 1)

            def body(b, parity, run, end):
                last = isinstance(b, int) and b == BATCHES - 1
                if run and not end:
                    for u in range(PASS_UNITS):
                        x_high(b, u)
                        if u < AHEAD:
                            w_high(b, u)
                asks, dones = (b - 1) * ASKS, (b - 1) * DONES
                for U in range(UNITS):
                    n, u = divmod(U, PASS_UNITS)
                    if u == 0 and (n > 0 and run or n == 0 and end):
                        tile_of_previous_pass(b, parity, n, TILES - 1)
                    if run and U + AHEAD < UNITS:
                        w_high(b, U + AHEAD)
                    elif run and not last:
                        w_high(b + 1, U + AHEAD - UNITS)
                    for k in turned_jobs(SPLIT_AT, n, u):
                        if n > 0 and run or n == 0 and end:
                            split_turned((b * STREAMS + n - 1) * TILES + k)
                    if end and U == STATS_AT - 1:
                        act.wait_ge(project_done, b * STREAMS * TILES)
                        nc.scalar.activation(xpre[0:2 * NLOGIT, :], logit_ps[0:2 * NLOGIT, :],
                                             ACT.Copy).then_inc(logit_copied, 1)
                    if end and run and U < 2:
                        x_high(b, PASS_UNITS - 2 + U)
                    if run and not last and U >= 3 * PASS_UNITS + 2:
                        x_high(b + 1, U - 3 * PASS_UNITS - 2)
                    if U == 0 and run and not end:
                        act.wait_ge(wall_in, 16)
                        nc.scalar.activation(wall_sb[:, :, 0:NLOGIT], wall_raw, ACT.Copy
                                             ).then_inc(const_hi, 1)
                        act.wait_ge(wb_in, 16)
                        nc.scalar.activation(wb_sb[:, 0, :, :], wb_raw, ACT.Copy
                                             ).then_inc(const_hi, 1)
                        act.wait_ge(base_in, 16)
                        nc.scalar.activation(gate[:, 0:1], base_sb[:, GATE:GATE + 1], ACT.Exp,
                                             scale=-1.0).then_inc(gate_exp, 1)
                    if end and U == STATS_AT:
                        answer(asks + 1, vec[:, 1, 0:TILES], vec[:, 0, 0:TILES], ACT.Ln)
                        act.wait_ge(act_done, dones + 1)
                        nc.scalar.activation(vec[:, 2, 0:TILES], vec[:, 1, 0:TILES], ACT.Exp,
                                             scale=-0.5).then_inc(act_done, 1)
                        heads = logit[:, :, NRES:NLOGIT]
                        answer(asks + 2, heads, heads, ACT.Exp)
                    if end and U in BLOCK_AT:
                        ask = asks + (3 if U == BLOCK_AT[0] else 6)
                        if U == BLOCK_AT[1]:
                            answer(ask, vec[:, LOG, :], vec[:, SUM, :], ACT.Ln)
                            ask = ask + 1
                        answer(ask, work[:], work[:], ACT.Exp)
                        answer(ask + 1, vec[:, LOG, :], vec[:, SUM, :], ACT.Ln)
                        answer(ask + 2, work[:], work[:], ACT.Exp)
                    for t in range(TILES):
                        if end and U == PRE_SPLIT_AT[t]:
                            act.wait_ge(pre_turned, (b - 1) * TILES + t + 1)
                            if t > 0:
                                act.wait_ge(y_ready, (b - 1) * TILES + t)
                            nc.scalar.activation(xpre_t[:, 0, :], y_ps[t % 2][:], ACT.Copy
                                                 ).then_inc(pre_hi_ready, 1)
                    if run and u == PASS_UNITS - 1:
                        for t in range(TILES - 1):
                            evacuate(b, parity, n, t)

            batches(act, body)

        @block.vector
        def _(dve):
            def w_low(b, unit):
                dve.wait_ge(w_hi_ready, b * UNITS + unit + 1)
                lo, hi = unit % LO_SLOTS, unit % HI_SLOTS
                nc.vector.tensor_tensor(w_lo[:, lo, :, :], w_raw[:, lo, :, :],
                                        w_hi[:, hi, :, :].bitcast(F32), ALU.subtract
                                        ).then_inc(w_lo_vector, 1)

            def x_low(b, u):
                dve.wait_ge(x_hi_ready, b * PASS_UNITS + u + 1)
                ks = slice(2 * u, 2 * u + 2)
                nc.vector.tensor_tensor(x_lo[:, ks, :], x_raw[:, ks, :],
                                        x_hi[:, ks, :].bitcast(F32), ALU.subtract
                                        ).then_inc(x_lo_ready, 1)

            def constants():
                dve.wait_ge(const_hi, 2)
                nc.vector.tensor_tensor(wall_sb[:, :, NLOGIT:2 * NLOGIT], wall_raw,
                                        wall_sb[:, :, 0:NLOGIT].bitcast(F32), ALU.subtract
                                        ).then_inc(const_ready, 1)
                nc.vector.tensor_tensor(wb_sb[:, 1, :, :], wb_raw,
                                        wb_sb[:, 0, :, :].bitcast(F32), ALU.subtract
                                        ).then_inc(const_ready, 1)
                dve.wait_ge(ident_ready, 1)
                nc.vector.tensor_tensor(pair_sum[:], ident[0:2 * NLOGIT, 0:NLOGIT],
                                        ident[0:2 * NLOGIT, NLOGIT:2 * NLOGIT], ALU.add
                                        ).then_inc(const_ready, 1)
                dve.wait_ge(gate_exp, 1)
                nc.vector.tensor_scalar(gate[:, 1:2], gate[:, 0:1], 1.0, None, ALU.add
                                        ).then_inc(gate_ready, 1)
                dve.wait_ge(gate_ready, 1)
                nc.vector.reciprocal(gate[:, 1:2], gate[:, 1:2]).then_inc(gate_ready, 1)
                dve.wait_ge(gate_ready, 2)
                nc.vector.tensor_scalar(gate[:, 2:3], gate[:, 1:2], -1.0, 1.0, ALU.mult,
                                        ALU.add).then_inc(mixed, 1)
                dve.wait_ge(mixed, 1)

            def turned_low(job):
                dve.wait_ge(cond_hi_ready, job + 1)
                nc.vector.tensor_tensor(cond_t[:, 1, :], turn_ps[:],
                                        cond_t[:, 0, :].bitcast(F32), ALU.subtract
                                        ).then_inc(cond_lo_ready, 1)

            def body(b, parity, run, end):
                first = not end
                last = isinstance(b, int) and b == BATCHES - 1
                c = b - 1
                count = [0]

                def mark(ins):
                    ins.then_inc(step, 1)
                    count[0] += 1
                    return count[0]

                def after(number):
                    dve.wait_ge(step, c * DVE_STEPS + number)

                def link(ins):
                    after(mark(ins))

                asked = [0, 0]

                def ask(ins, dones=1):
                    ins.then_inc(act_ask, 1)
                    asked[1] += dones
                    dve.wait_ge(act_done, c * DONES + asked[1])

                tt, reduce = nc.vector.tensor_tensor, nc.vector.tensor_reduce
                by_row = "p (t i j) -> p t i j"
                work_r = work[:].rearrange(by_row, i=STREAMS, j=STREAMS)
                work_c = work[:].rearrange("p (t i j) -> p t j i", i=STREAMS, j=STREAMS)
                kern_r = kern[:].rearrange(by_row, i=STREAMS, j=STREAMS)
                kern_c = kern[:].rearrange("p (t i j) -> p t j i", i=STREAMS, j=STREAMS)
                z_r = logit[:, :, 0:NRES].rearrange("p t (i j) -> p t i j", j=STREAMS)

                def small(k):
                    return vec[:, k, :].rearrange("p (t i) -> p t i", i=STREAMS)

                def over_rows(k):
                    return small(k).unsqueeze(3).to_broadcast([P, TILES, STREAMS, STREAMS])

                def over_columns(k):
                    return small(k).unsqueeze(2).to_broadcast([P, TILES, STREAMS, STREAMS])

                def statistics():
                    dve.wait_ge(acc_free, b * STREAMS * TILES)
                    link(reduce(vec[:, 0, 0:TILES], ssq[:], AX, ALU.add))
                    ask(nc.vector.tensor_scalar(vec[:, 0, 0:TILES], vec[:, 0, 0:TILES], 1.0 / DIM,
                                                RMS_EPS, ALU.mult, ALU.add), dones=2)
                    ms, r0, t = vec[:, 0, 0:TILES], vec[:, 2, 0:TILES], vec[:, 4, 0:TILES]
                    link(tt(t, r0, r0, ALU.mult))
                    link(tt(t, t, ms, ALU.mult))
                    link(nc.vector.tensor_scalar(t, t, -0.5, 1.5, ALU.mult, ALU.add))
                    link(tt(vec[:, 5, 0:TILES], r0, t, ALU.mult))
                    dve.wait_ge(logit_gathered, b)
                    tt(logit[:], turn_ps[:, 0:TILES * NLOGIT].rearrange(
                        "p (t l) -> p t l", l=NLOGIT),
                       vec[:, 5, 0:TILES].unsqueeze(2).to_broadcast([P, TILES, NLOGIT]),
                       ALU.mult).then_inc(stats_read, 1)
                    dve.wait_ge(stats_read, b)
                    link(tt(logit[:], logit[:],
                            base_sb[:, 0:NLOGIT].unsqueeze(1).to_broadcast([P, TILES, NLOGIT]),
                            ALU.add))
                    heads = logit[:, :, NRES:NLOGIT].rearrange("p t (h j) -> p t h j", j=STREAMS)
                    eight = vec[:, 0:2, :].rearrange("p k f -> p (k f)")[:, 0:2 * TILES]
                    head = eight.rearrange("p (t h) -> p t h", h=2)
                    head_b = head.unsqueeze(3).to_broadcast([P, TILES, 2, STREAMS])
                    link(reduce(head, heads, AX, ALU.max))
                    ask(tt(heads, heads, head_b, ALU.subtract))
                    link(reduce(head, heads, AX, ALU.add))
                    link(nc.vector.reciprocal(eight, eight))
                    link(tt(heads, heads, head_b, ALU.mult))
                    z = logit[:, :, 0:NRES]
                    link(nc.vector.tensor_scalar(z, z, 1.0 / TAU, None, ALU.mult))

                def log_step(k):
                    if k == 0:
                        source = z_r
                    else:
                        ask(tt(vec[:, SUM, :], vec[:, B, :], vec[:, INV, :], ALU.mult))
                        link(tt(vec[:, COLMAX, :], vec[:, LOG, :], vec[:, COLMAX, :],
                                ALU.subtract))
                        link(tt(work_r, z_r, over_columns(COLMAX), ALU.add))
                        source = work_r
                    link(reduce(small(ROWMAX), source, AX, ALU.max))
                    ask(tt(work_r, source, over_rows(ROWMAX), ALU.subtract))
                    ask(reduce(small(SUM), work_r, AX, ALU.add))
                    link(tt(vec[:, ROWMAX, :], vec[:, ROWMAX, :], vec[:, LOG, :], ALU.add))
                    link(tt(work_r, z_r, over_rows(ROWMAX), ALU.subtract))
                    link(reduce(small(COLMAX), work_c, AX, ALU.max))
                    ask(tt(work_r, work_r, over_columns(COLMAX), ALU.subtract))
                    link(reduce(small(INV), work_c, AX, ALU.add))
                    link(nc.vector.reciprocal(vec[:, INV, :], vec[:, INV, :]))
                    link(tt(kern_r, work_r, over_columns(INV), ALU.mult))
                    link(tt(work_r, work_r, over_columns(INV), ALU.mult))

                def fast_step():
                    link(reduce(small(A), work_r, AX, ALU.add))
                    link(nc.vector.reciprocal(vec[:, A, :], vec[:, A, :]))
                    link(tt(work_r, kern_r, over_rows(A), ALU.mult))
                    link(reduce(small(B), work_c, AX, ALU.add))
                    link(nc.vector.reciprocal(vec[:, B, :], vec[:, B, :]))
                    link(tt(work_r, kern_r, over_columns(B), ALU.mult))

                def final_matrix():
                    link(tt(kern_r, work_r, over_rows(A), ALU.mult))
                    link(nc.vector.tensor_scalar(kern[:], kern[:], gate[:, 1:2], None, ALU.mult))
                    diagonal = kern[:].rearrange("p (t f) -> p t f", f=NRES)[
                        :, :, 0:NRES:STREAMS + 1]
                    link(nc.vector.tensor_scalar(diagonal, diagonal, gate[:, 2:3], None, ALU.add))

                def pre(t):
                    if t > 0:
                        dve.wait_ge(pre_turned, c * TILES + t)
                    for j in range(STREAMS):
                        weight = logit[:, t, NRES + j:NRES + j + 1]
                        source = cond[:, 1 - parity, j, t, :]
                        if j == 0:
                            link(nc.vector.tensor_scalar(xpre[:], source, weight, None, ALU.mult))
                            continue
                        ins = nc.vector.scalar_tensor_tensor(
                            out=xpre[:], in0=source, scalar=weight, in1=xpre[:],
                            op0=ALU.mult, op1=ALU.add)
                        if j < STREAMS - 1:
                            link(ins)
                        else:
                            ins.then_inc(pre_ready, 1)

                def pre_low(t):
                    dve.wait_ge(pre_hi_ready, c * TILES + t + 1)
                    nc.vector.tensor_tensor(xpre_t[:, 1, :], y_ps[t % 2][:],
                                            xpre_t[:, 0, :].bitcast(F32), ALU.subtract
                                            ).then_inc(pre_lo_ready, 1)

                def mix(t, p):
                    q = 2 * t + p
                    slot = q % OUT_SLOTS
                    dve.wait_ge(residual_in[slot], (c * 2 + q // OUT_SLOTS + 1) * 16)
                    written = [0, 0]
                    for j in range(STREAMS + 1):
                        for s in range(2):
                            i = 2 * p + s
                            if j < STREAMS:
                                source = cond[:, 1 - parity, j, t, :]
                                weight = kern[:, t * NRES + i * STREAMS + j:][:, 0:1]
                            else:
                                source = y_ps[t % 2][:]
                                weight = logit[:, t, NRES + STREAMS + i:][:, 0:1]
                                if s == 0:
                                    dve.wait_ge(y_ready, c * TILES + t + 1)
                            if j > 0:
                                after(written[s])
                            ins = nc.vector.scalar_tensor_tensor(
                                out=piece[:, slot, s, :], in0=source, scalar=weight,
                                in1=piece[:, slot, s, :], op0=ALU.mult, op1=ALU.add)
                            if j == STREAMS and s == 1:
                                ins.then_inc(mixed, 1)
                            else:
                                written[s] = mark(ins)

                if first:
                    for u in range(PASS_UNITS):
                        x_low(b, u)
                        if u < AHEAD:
                            w_low(b, u)
                for U in range(UNITS):
                    n, u = divmod(U, PASS_UNITS)
                    if run and U + AHEAD in VECTOR_SUBS:
                        w_low(b, U + AHEAD)
                    if run and not last and U + AHEAD >= UNITS:
                        w_low(b + 1, U + AHEAD - UNITS)
                    if first and U == 0:
                        constants()
                    for k in turned_jobs(SPLIT_AT, n, u):
                        if n > 0 and run or n == 0 and end:
                            turned_low((b * STREAMS + n - 1) * TILES + k)
                    if not end:
                        continue
                    if U == STATS_AT:
                        statistics()
                    for t in range(TILES):
                        if U == PRE_SPLIT_AT[t]:
                            pre_low(t)
                    for k in range(BLOCKS):
                        if U == BLOCK_AT[k]:
                            log_step(k)
                        start, stop = FAST_AT[k]
                        if start <= U < stop:
                            for _ in range(FAST * (U - start) // (stop - start),
                                           FAST * (U + 1 - start) // (stop - start)):
                                fast_step()
                    if U == FINAL_AT:
                        final_matrix()
                    for q in range(MIX_PAIRS):
                        if U == MIX_AT[q]:
                            mix(q // 2, q % 2)
                    for t in range(TILES):
                        if U == PRE_AT[t]:
                            pre(t)
                if end:
                    assert count[0] == DVE_STEPS, count[0]

            batches(dve, body)

        @block.tensor
        def _(pe):
            def half_unit(b, U, half):
                n, u = divmod(U, PASS_UNITS)
                if half:
                    pass
                elif U in VECTOR_SUBS:
                    pe.wait_ge(w_lo_vector, b * VS + VECTOR_SUBS.index(U) + 1)
                else:
                    pe.wait_ge(w_lo_gpsimd, b * GS + GPSIMD_SUBS.index(U) + 1)
                if n == 0 and not half:
                    pe.wait_ge(x_lo_ready, b * PASS_UNITS + u + 1)
                for t in range(half * TILES // 2, (half + 1) * TILES // 2):
                    if u == 0 and not (n == 0 and isinstance(b, int) and b == 0):
                        pe.wait_ge(acc_free, (b * STREAMS + n - 1) * TILES + t + 1)
                    rows = slice(t * P, (t + 1) * P)
                    for k in range(UNIT_CHUNKS):
                        chunk = UNIT_CHUNKS * u + k
                        wh, wl = w_hi[:, U % HI_SLOTS, k, :], w_lo[:, U % LO_SLOTS, k, :]
                        xh, xl = x_hi[:, chunk, rows], x_lo[:, chunk, rows]
                        for m, (stationary, moving) in enumerate(((xh, wh), (xh, wl), (xl, wh))):
                            mm = nc.tensor.matmul(acc[t][:], stationary, moving,
                                                  start=(chunk == 0 and m == 0),
                                                  stop=(chunk == CHUNKS - 1 and m == 2))
                    if u == PASS_UNITS - 1:
                        mm.then_inc(acc_done, 1)
                if half and u < PASS_UNITS - 1:
                    mm.then_inc(unit_done, 1)

            def turn(source, plane_job, k):
                if k == 0:
                    pe.wait_ge(cond_ready, plane_job + TILES)
                if not (isinstance(plane_job, int) and plane_job + k == 0):
                    pe.wait_ge(cond_lo_ready, plane_job + k)
                for t in range(TILES):
                    mm = nc.tensor.transpose(turn_ps[:, t * P:(t + 1) * P],
                                             source[:, t, k * P:(k + 1) * P], ident[:])
                mm.then_inc(turn_done, 1)

            def project(n, k, job):
                pe.wait_ge(cond_lo_ready, job + 1)
                chunk = n * (C // P) + k
                nc.tensor.matmul(logit_ps[0:2 * NLOGIT, :], wall_sb[:, chunk, :],
                                 cond_t[:, 0, :], start=(chunk == 0), stop=False,
                                 skip_group_check=True)
                mm = nc.tensor.matmul(logit_ps[0:NLOGIT, :], wall_sb[:, chunk, 0:NLOGIT],
                                      cond_t[:, 1, :], start=False, stop=(chunk == CHUNKS - 1),
                                      skip_group_check=True)
                mm.then_inc(project_done, 1)

            def gather(b):
                pe.wait_ge(logit_copied, b)
                for t in range(TILES):
                    mm = nc.tensor.matmul(turn_ps[:, t * NLOGIT:(t + 1) * NLOGIT],
                                          xpre[0:2 * NLOGIT, t * P:(t + 1) * P], pair_sum[:],
                                          start=True, stop=True)
                mm.then_inc(logit_gathered, 1)

            def turn_pre(c, t):
                tile = c * TILES + t
                pe.wait_ge(pre_ready, tile + 1)
                pe.wait_ge(mixed, 1 + c * MIX_PAIRS + max(0, t - 1) * 2)
                for k in range(C // P):
                    cols = slice(k * P, (k + 1) * P)
                    mm = nc.tensor.transpose(y_ps[t % 2][:, cols], xpre[:, cols], ident[:])
                mm.then_inc(pre_turned, 1)

            def branch(c, t):
                pe.wait_ge(pre_lo_ready, c * TILES + t + 1)
                for k in range(C // P):
                    cols = slice(k * P, (k + 1) * P)
                    high, low = xpre_t[:, 0, cols], xpre_t[:, 1, cols]
                    for m, (stationary, half) in enumerate(((high, 0), (high, 1), (low, 0))):
                        mm = nc.tensor.matmul(y_ps[t % 2][:], stationary, wb_sb[:, half, k, :],
                                              start=(k == 0 and m == 0),
                                              stop=(k == C // P - 1 and m == 2))
                mm.then_inc(y_ready, 1)

            def body(b, parity, run, end):
                for H in range(2 * UNITS):
                    U, half = divmod(H, 2)
                    n = U // PASS_UNITS
                    if run:
                        half_unit(b, U, half)
                    if n > 0 and run or n == 0 and end:
                        job = (b * STREAMS + n - 1) * TILES
                        plane, side = (n - 1, parity) if n > 0 else (STREAMS - 1, 1 - parity)
                        at = H % (2 * PASS_UNITS)
                        for k in turned_jobs(PROJECT_AT, n, at):
                            project(plane, k, job + k)
                        for k in turned_jobs(TURN_AT, n, at):
                            if n == 1 and k == 0 and not end:
                                pe.wait_ge(ident_ready, 1)
                                pe.wait_ge(const_ready, 3)
                            if n == 1 and k == 0 and end:
                                pe.wait_ge(stats_read, b)
                            turn(cond[:, side, plane, :, :], job, k)
                    if end and H == GATHER_AT:
                        gather(b)
                    for t in range(TILES):
                        if end and half and U == PRE_T_AT[t]:
                            turn_pre(b - 1, t)
                        if end and half and U == Y_AT[t]:
                            branch(b - 1, t)

            batches(pe, body)


def kernel(x, itok_B_3_7, L0_cond_weight, L0_ffn_W_res, L0_ffn_W_pre, L0_ffn_W_post,
           L0_ffn_H_res_base, L0_ffn_H_pre_base, L0_ffn_H_post_base, L0_ffn_gate, L0_ffn_W_branch):
    import concourse.bacc as bacc
    from concourse.bass_utils import run_bass_kernel_spmd

    x = np.asarray(x)
    weight = np.asarray(L0_cond_weight)
    xt = x.reshape(BATCHES, TOKENS, PASS_UNITS, UNIT_CHUNKS, P).transpose(0, 2, 4, 3, 1)
    wt = weight.reshape(ADAPTERS, STREAMS, C, PASS_UNITS, UNIT_CHUNKS, P)
    wt = wt.transpose(0, 1, 3, 5, 4, 2)
    xn = x.reshape(BATCHES, TILES, P, 2, 2 * C).transpose(0, 1, 3, 2, 4)
    wall = np.concatenate([np.asarray(w) for w in (L0_ffn_W_res, L0_ffn_W_pre, L0_ffn_W_post)])
    base = np.concatenate([np.asarray(v).reshape(-1) for v in (
        L0_ffn_H_res_base, L0_ffn_H_pre_base, L0_ffn_H_post_base, L0_ffn_gate)])
    arrays = {
        "xt": xt.reshape(BATCHES * PASS_UNITS, P, UNIT_CHUNKS * TOKENS),
        "xn": xn.reshape(BATCHES * MIX_PAIRS, P, 2 * C),
        "wt": wt.reshape(ADAPTERS * UNITS, P, UNIT_CHUNKS * C),
        "ids": np.asarray(itok_B_3_7).reshape(1, BATCHES),
        "wall": wall.reshape(NLOGIT, CHUNKS, P).transpose(2, 1, 0),
        "base": base.reshape(1, NLOGIT + 1),
        "wb": np.asarray(L0_ffn_W_branch).reshape(C // P, P, C).transpose(1, 0, 2),
    }
    arrays = {name: np.ascontiguousarray(a) for name, a in arrays.items()}
    nc = bacc.Bacc("TRN2", target_bir_lowering=False, num_devices=1)
    args = [nc.dram_tensor(name, a.shape, mybir.dt.from_np(a.dtype), kind="ExternalInput").ap()
            for name, a in arrays.items()]
    out = nc.dram_tensor("out", (BATCHES * MIX_PAIRS, P, 2 * C), F32, kind="ExternalOutput").ap()
    build(nc, *args, out)
    got = run_bass_kernel_spmd(nc, [arrays], core_ids=[0]).results[0]["out"]
    got = got.reshape(BATCHES, TILES, 2, P, 2 * C).transpose(0, 1, 3, 2, 4)
    return np.ascontiguousarray(got.reshape(BATCHES, TOKENS, DIM))
```

```python
from contextlib import ExitStack

import numpy as np

import concourse.bass as bass
from concourse import mybir

F32 = mybir.dt.float32
F32R = mybir.dt.float32r
I32 = mybir.dt.int32
ACT = mybir.ActivationFunctionType
ALU = mybir.AluOpType
AX = mybir.AxisListType.X

P = 128
BATCHES, TOKENS, DIM = 8, 512, 2048
ADAPTERS = 8
STREAMS = 4
C = DIM // STREAMS
TILES = TOKENS // P
CHUNKS = DIM // P
UNIT_CHUNKS = 2
PASS_UNITS = CHUNKS // UNIT_CHUNKS
UNITS = STREAMS * PASS_UNITS
LO_SLOTS = 4
HI_SLOTS = 4
AHEAD = 2
NRES = STREAMS * STREAMS
NLOGIT = NRES + 2 * STREAMS
GATE = NLOGIT
MIX_PAIRS = TILES * 2
OUT_SLOTS = 4
RMS_EPS = 1.1920929e-07
TAU = 0.1
BLOCKS = 2
FAST = 24

FIRST_X = 3
CONSTANTS_AT = 6
WARM_UP = 40

VECTOR_SUBS = (0, 1)
GPSIMD_SUBS = tuple(U for U in range(UNITS) if U not in VECTOR_SUBS)
VS, GS = len(VECTOR_SUBS), len(GPSIMD_SUBS)

TURN_AT = {True: (0, 1, 2, 3), False: (1, 5, 8, 11)}
PROJECT_AT = {True: (1, 2, 3, 4), False: (4, 8, 11, 15)}
SPLIT_AT = {True: (0, 0, 1, 1), False: (1, 3, 4, 6)}
GATHER_AT = 5

RMS_AT = 0
STATS_AT = 3
BLOCK_AT = (3, 12)
FAST_AT = ((5, 12), (13, 20))
FINAL_AT = 20
PRE_AT = (8, 12, 16, 24)
PRE_T_AT = (10, 14, 23, 26)
PRE_SPLIT_AT = (11, 15, 24, 27)
Y_AT = (13, 17, 25, 28)
MIX_AT = (21, 22, 24, 25, 26, 27, 29, 30)
RESIDUAL_AT = (14, 15, 16, 17, 24, 25, 26, 27)
STORE_AT = (23, 24, 26, 27, 28, 29, 31, 31)
DVE_STEPS = 404
ASKS, DONES = 9, 10
END_VECTOR = (((0, 0), (0, 1)), ((1, 0), (1, 1)), ((2, 0), (2, 1)), ((3, 0),))
END_TENSOR = ((0, 2), (1, 2), (2, 2), (3, 1), (3, 2))
END_GPSIMD_TERMS = TILES * STREAMS - 2
ROWMAX, LOG, SUM, COLMAX, A, B, INV = range(7)


def build(nc, xt, xn, wt, ids, wall, base, wb, out):
    ctx = ExitStack()
    with ctx:
        def sb(name, shape, dt=F32):
            return ctx.enter_context(nc.sbuf_tensor(name, shape, dt))

        def ps(name, shape):
            return ctx.enter_context(nc.psum_tensor(name, shape, F32))

        def sem(name):
            return ctx.enter_context(nc.semaphore(name))

        def raw_and_low(name, shape):
            place = nc.sbuf_base
            raw = sb(name + "_raw", shape)
            assert nc.sbuf_base - place == int(np.prod(shape[1:])) * 4
            return raw, nc.alloc_sbuf_tensor_at(name + "_lo", shape, F32R, offset=place)

        x_hi = sb("x_hi", [P, CHUNKS, TOKENS], F32R)
        x_raw, x_lo = raw_and_low("x", [P, CHUNKS, TOKENS])
        w_raw, w_lo = raw_and_low("w", [P, LO_SLOTS, UNIT_CHUNKS, C])
        w_hi = sb("w_hi", [P, HI_SLOTS, UNIT_CHUNKS, C], F32R)
        cond = sb("cond", [P, 2, STREAMS, TILES, C])
        piece = sb("piece", [P, OUT_SLOTS, 2, C])
        cond_t = sb("cond_t", [P, 2, TOKENS], F32R)
        xpre = sb("xpre", [P, C])
        xpre_t = sb("xpre_t", [P, 2, C], F32R)
        wall_sb = sb("wall_sb", [P, CHUNKS, 2 * NLOGIT], F32R)
        wb_sb = sb("wb_sb", [P, 2, C // P, C], F32R)
        wall_raw = cond[:, 1, 0, :, :].rearrange("p t c -> p (t c)")[:, 0:CHUNKS * NLOGIT]
        wall_raw = wall_raw.rearrange("p (k l) -> p k l", l=NLOGIT)
        wb_raw = cond[:, 1, 1, :, :]
        ident = sb("ident", [P, P])
        pair_sum = sb("pair_sum", [2 * NLOGIT, NLOGIT])
        base_sb = sb("base_sb", [P, NLOGIT + 1])
        logit = sb("logit", [P, TILES, NLOGIT])
        kern = sb("kern", [P, TILES * NRES])
        work = sb("work", [P, TILES * NRES])
        vec = sb("vec", [P, 7, TILES * STREAMS])
        ssq = sb("ssq", [P, TILES, STREAMS])
        gate = sb("gate", [P, 3])

        end_out = x_raw
        end_c, end_term = cond[:, 1, :, :, :], cond[:, 0, :, :, :]
        end_diagonal = w_raw[:].rearrange("p s k c -> p (s k) c")
        assert BATCHES % 2 == 0 and CHUNKS == TILES * STREAMS and LO_SLOTS * UNIT_CHUNKS >= len(END_TENSOR)

        acc = [ps(f"acc{t}", [P, C]) for t in range(TILES)]
        logit_ps = ps("logit_ps", [P, C])
        turn_ps = ps("turn_ps", [P, C])
        y_ps = [ps(f"y_ps{i}", [P, C]) for i in range(2)]

        end_bank = acc + [y_ps[0]]

        w_in = [sem(f"w_in{i}") for i in range(LO_SLOTS)]
        x_in = [sem(f"x_in{i}") for i in range(PASS_UNITS)]
        base_in, wall_in, wb_in = sem("base_in"), sem("wall_in"), sem("wb_in")
        const_hi, const_ready = sem("const_hi"), sem("const_ready")
        ident_zero, ident_ready = sem("ident_zero"), sem("ident_ready")
        w_hi_ready = sem("w_hi_ready")
        w_lo_vector, w_lo_gpsimd = sem("w_lo_vector"), sem("w_lo_gpsimd")
        x_hi_ready, x_lo_ready = sem("x_hi_ready"), sem("x_lo_ready")
        unit_done = sem("unit_done")
        acc_done = sem("acc_done")
        cond_ready = sem("cond_ready")
        acc_free = sem("acc_free")
        turn_done = sem("turn_done")
        cond_hi_ready, cond_lo_ready = sem("cond_hi_ready"), sem("cond_lo_ready")
        project_done = sem("project_done")
        logit_copied, logit_gathered = sem("logit_copied"), sem("logit_gathered")
        stats_read = sem("stats_read")
        act_ask, act_done = sem("act_ask"), sem("act_done")
        gate_exp, gate_ready = sem("gate_exp"), sem("gate_ready")
        pre_ready, pre_turned = sem("pre_ready"), sem("pre_turned")
        pre_hi_ready, pre_lo_ready = sem("pre_hi_ready"), sem("pre_lo_ready")
        y_ready = sem("y_ready")
        pre_weighed, pre_copied = sem("pre_weighed"), sem("pre_copied")
        y_weighed, base_added = sem("y_weighed"), sem("base_added")
        matrix_ready, diagonal_ready = sem("matrix_ready"), sem("diagonal_ready")
        terms_ready, terms_added = sem("terms_ready"), sem("terms_added")
        summed, summed_copied = sem("summed"), sem("summed_copied")
        step = sem("step")
        mixed = sem("mixed")
        residual_in = [sem(f"residual_in{i}") for i in range(OUT_SLOTS)]
        stored = [sem(f"stored{i}") for i in range(OUT_SLOTS)]

        block = ctx.enter_context(nc.Block())

        def wait_unit(eng, b, unit):
            n, u = divmod(unit, PASS_UNITS)
            if isinstance(b, int) and b * UNITS + unit < 0:
                return
            if u < PASS_UNITS - 1:
                eng.wait_ge(unit_done, (b * STREAMS + n) * (PASS_UNITS - 1) + u + 1)
            else:
                eng.wait_ge(acc_done, (b * STREAMS + n + 1) * TILES)

        def turned_jobs(plan, n, at):
            return [k for k, when in enumerate(plan[n == 0]) if when == at]

        def batches(eng, body, ending):
            body(0, 0, False)
            with eng.Fori(0, (BATCHES - 2) // 2) as i:
                body(i * 2 + 1, 1, True)
                body(i * 2 + 2, 0, True)
            body(BATCHES - 1, 1, True)
            ending()

        @block.sync
        def _(sp):
            def index(value):
                return value if isinstance(value, int) else sp.snap(value)

            def adapter_of(b):
                return sp.value_load(ids[0:1, bass.ds(b, 1)], min_val=0, max_val=ADAPTERS - 1)

            def load_weights(adapter, b, unit):
                slot = unit % LO_SLOTS
                place = index(adapter * UNITS + unit % UNITS)
                wait_unit(sp, b, unit - LO_SLOTS)
                sp.dma_start(w_raw[:, slot, :, :],
                             wt[bass.ds(place, 1), :, :]
                             .rearrange("a p (k c) -> (a p) k c", k=UNIT_CHUNKS)
                             ).then_inc(w_in[slot], 16)

            def load_x(b, u, pieces_of=None):
                place = index(b * PASS_UNITS + u)
                if pieces_of is not None:
                    count = index(pieces_of * 2 * 16)
                wait_unit(sp, b - 1, 3 * PASS_UNITS + u)
                if pieces_of is not None:
                    for slot in range(OUT_SLOTS):
                        sp.wait_ge(stored[slot], count)
                sp.dma_start(x_raw[:, 2 * u:2 * u + 2, :],
                             xt[bass.ds(place, 1), :, :]
                             .rearrange("a p (k s) -> (a p) k s", k=UNIT_CHUNKS)
                             ).then_inc(x_in[u], 16)

            def load_last_residual(q):
                wait_unit(sp, BATCHES - 1, 3 * PASS_UNITS + q)
                sp.dma_start(end_out[:, 2 * q:2 * q + 2, :], rows(xn, (BATCHES - 1) * MIX_PAIRS + q)
                             ).then_inc(x_in[q], 16)

            def ending():
                load_last_residual(MIX_PAIRS - 1)
                for q in range(MIX_PAIRS):
                    t, p = divmod(q, 2)
                    streams = [(t, 2 * p), (t, 2 * p + 1)]
                    for n, group in enumerate(END_VECTOR):
                        if group[0] in streams:
                            sp.wait_ge(mixed, 1 + (BATCHES - 1) * MIX_PAIRS + n + 1)
                    for n, stream in enumerate(END_TENSOR):
                        if stream in streams:
                            sp.wait_ge(summed_copied, n + 1)
                    if q == MIX_PAIRS - 1:
                        sp.wait_ge(mixed, 1 + (BATCHES - 1) * MIX_PAIRS + len(END_VECTOR) + 1)
                    elif p == 1:
                        sp.wait_ge(terms_added, (t + 1) * STREAMS)
                    sp.dma_start(rows(out, (BATCHES - 1) * MIX_PAIRS + q),
                                 end_out[:, 2 * q:2 * q + 2, :]).then_inc(stored[q % OUT_SLOTS], 16)

            def rows(t, place):
                return t[bass.ds(place, 1), :, :].rearrange("a p (s c) -> (a p) s c", s=2)

            def body(b, parity, end):
                last = isinstance(b, int) and b == BATCHES - 1
                adapter = adapter_of(b)
                if not end:
                    for u in range(PASS_UNITS):
                        load_x(b, u)
                        if u < AHEAD + 2:
                            load_weights(adapter, b, u)
                        if u == 0:
                            sp.dma_start(base_sb[:], base.to_broadcast([P, NLOGIT + 1])
                                         ).then_inc(base_in, 16)
                    sp.dma_start(wall_raw, wall).then_inc(wall_in, 16)
                    sp.dma_start(wb_raw, wb).then_inc(wb_in, 16)
                else:
                    load_x(b, PASS_UNITS - 1)
                for U in range(UNITS):
                    unit = U + AHEAD + 1
                    if unit < UNITS and (end or U > 0):
                        load_weights(adapter, b, unit)
                    if not last:
                        if unit == UNITS - 1:
                            following = adapter_of(b + 1)
                        if unit >= UNITS:
                            load_weights(following, b, unit)
                    for q in range(MIX_PAIRS):
                        slot, use = q % OUT_SLOTS, q // OUT_SLOTS
                        if end and U == STORE_AT[q]:
                            place = index((b - 1) * MIX_PAIRS + q)
                            sp.wait_ge(mixed, 1 + (b - 1) * MIX_PAIRS + q + 1)
                            sp.dma_start(rows(out, place), piece[:, slot, :, :]
                                         ).then_inc(stored[slot], 16)
                        if end and U == RESIDUAL_AT[q]:
                            place = index((b - 1) * MIX_PAIRS + q)
                            if use > 0:
                                sp.wait_ge(stored[slot], ((b - 1) * 2 + 1) * 16)
                            sp.dma_start(piece[:, slot, :, :], rows(xn, place)
                                         ).then_inc(residual_in[slot], 16)
                    if not last and U > 3 * PASS_UNITS:
                        load_x(b + 1, U - 3 * PASS_UNITS - 1,
                               pieces_of=b if end and U == UNITS - 1 else None)
                    if last and U > 3 * PASS_UNITS:
                        load_last_residual(U - 3 * PASS_UNITS - 1)

            batches(sp, body, ending)
            for slot in range(OUT_SLOTS):
                sp.wait_ge(stored[slot], BATCHES * 2 * 16)

        @block.gpsimd
        def _(pool):
            nc.gpsimd.memset(ident[:], 0.0).then_inc(ident_zero, 1)
            pool.wait_ge(ident_zero, 1)
            nc.gpsimd.affine_select(out=ident[:], in_=ident[:], compare_op=ALU.not_equal,
                                    fill=1.0, base=0, pattern=[[-1, P]],
                                    channel_multiplier=1).then_inc(ident_ready, 1)

            def w_low(b, unit):
                pool.wait_ge(w_hi_ready, b * UNITS + unit + 1)
                lo, hi = unit % LO_SLOTS, unit % HI_SLOTS
                nc.gpsimd.tensor_tensor(w_lo[:, lo, :, :], w_raw[:, lo, :, :],
                                        w_hi[:, hi, :, :].bitcast(F32), ALU.subtract
                                        ).then_inc(w_lo_gpsimd, 1)

            def x_low(b, u):
                pool.wait_ge(x_hi_ready, b * PASS_UNITS + u + 1)
                ks = slice(2 * u, 2 * u + 2)
                nc.gpsimd.tensor_tensor(x_lo[:, ks, :], x_raw[:, ks, :],
                                        x_hi[:, ks, :].bitcast(F32), ALU.subtract
                                        ).then_inc(x_lo_ready, 1)

            def ending():
                first_tile = (BATCHES - 1) * TILES

                def pre_low(t):
                    pool.wait_ge(pre_hi_ready, first_tile + t + 1)
                    pool.wait_ge(pre_copied, t + 1)
                    nc.gpsimd.tensor_tensor(xpre_t[:, 1, :], xpre[:],
                                            xpre_t[:, 0, :].bitcast(F32), ALU.subtract
                                            ).then_inc(pre_lo_ready, 1)

                def add_y(t):
                    for i in range(STREAMS):
                        plane = t * STREAMS + i
                        pool.wait_ge(x_in[plane // 2], (BATCHES + 1) * 16)
                        pool.wait_ge(y_weighed, plane + 1)
                        nc.gpsimd.tensor_tensor(end_out[:, plane, :], end_out[:, plane, :],
                                                end_term[:, i, t, :], ALU.add
                                                ).then_inc(base_added, 1)

                def mix_stream(t):
                    plane = (t + 1) * STREAMS - 1
                    pool.wait_ge(base_added, plane + 1)
                    for j in range(min(STREAMS, END_GPSIMD_TERMS - t * STREAMS)):
                        pool.wait_ge(terms_ready, t * STREAMS + j + 1)
                        if j > 0:
                            pool.wait_ge(terms_added, t * STREAMS + j)
                        nc.gpsimd.tensor_tensor(end_out[:, plane, :], end_out[:, plane, :],
                                                end_term[:, j, t, :], ALU.add
                                                ).then_inc(terms_added, 1)

                pre_low(0)
                for t in range(TILES):
                    if t + 1 < TILES:
                        pre_low(t + 1)
                    add_y(t)
                for t in range(TILES):
                    mix_stream(t)

            def body(b, parity, end):
                last = isinstance(b, int) and b == BATCHES - 1
                for U in range(UNITS):
                    if U + AHEAD in GPSIMD_SUBS:
                        w_low(b, U + AHEAD)
                    if end and U < 2:
                        x_low(b, PASS_UNITS - 2 + U)
                    if U >= 3 * PASS_UNITS + 2 and not last:
                        x_low(b + 1, U - 3 * PASS_UNITS - 2)

            batches(pool, body, ending)

        @block.scalar
        def _(act):
            nc.scalar.preload_act_table_set("natural_log_exp_and_others")

            def w_high(b, unit):
                act.wait_ge(w_in[unit % LO_SLOTS],
                            (b * (UNITS // LO_SLOTS) + unit // LO_SLOTS + 1) * 16)
                wait_unit(act, b, unit - HI_SLOTS)
                nc.scalar.activation(w_hi[:, unit % HI_SLOTS, :, :],
                                     w_raw[:, unit % LO_SLOTS, :, :], ACT.Copy
                                     ).then_inc(w_hi_ready, 1)

            def x_high(b, u):
                act.wait_ge(x_in[u], (b + 1) * 16)
                ks = slice(2 * u, 2 * u + 2)
                nc.scalar.activation(x_hi[:, ks, :], x_raw[:, ks, :], ACT.Copy
                                     ).then_inc(x_hi_ready, 1)

            def evacuate(b, parity, n, t):
                done = (b * STREAMS + n) * TILES + t + 1
                act.wait_ge(acc_done, done)
                if n == 0 and t == 0 and not (isinstance(b, int) and b == 0):
                    act.wait_ge(stats_read, b)
                if n == 0 and not (isinstance(b, int) and b < 2):
                    act.wait_ge(mixed, 1 + (b - 1) * MIX_PAIRS)
                nc.scalar.activation(cond[:, parity, n, t, :], acc[t][:], ACT.Copy
                                     ).then_inc(cond_ready, 1)
                act.wait_ge(cond_ready, done)
                nc.scalar.activation(acc[t][:], acc[t][:], ACT.Square,
                                     accum_out=ssq[:, t, n:n + 1]).then_inc(acc_free, 1)

            def tile_of_previous_pass(b, parity, n, t):
                if n > 0:
                    evacuate(b, parity, n - 1, t)
                else:
                    evacuate(b - 1, 1 - parity, STREAMS - 1, t)

            def ending():
                b, c = BATCHES, BATCHES - 1
                first_tile, job = c * TILES, (BATCHES * STREAMS - 1) * TILES
                asks, dones = c * ASKS, c * DONES

                def weigh(o, i, weight, signal):
                    nc.scalar.activation(o, i, ACT.Copy, scale=weight).then_inc(signal, 1)

                def split_pre(t):
                    act.wait_ge(pre_turned, first_tile + t + 1)
                    if t > 0:
                        act.wait_ge(y_ready, first_tile + t)
                    nc.scalar.activation(xpre_t[:, 0, :], y_ps[t % 2][:], ACT.Copy
                                         ).then_inc(pre_hi_ready, 1)
                    if t > 0:
                        act.wait_ge(pre_lo_ready, first_tile + t)
                    nc.scalar.activation(xpre[:], y_ps[t % 2][:], ACT.Copy
                                         ).then_inc(pre_copied, 1)

                def weigh_streams(t):
                    for j in range(STREAMS):
                        weigh(end_term[:, j, t, :], end_c[:, j, t, :],
                              logit[:, t, NRES + j:NRES + j + 1], pre_weighed)

                def weigh_y(t):
                    act.wait_ge(y_ready, first_tile + t + 1)
                    for i in range(STREAMS):
                        weigh(end_term[:, i, t, :], acc[t][:],
                              logit[:, t, NRES + STREAMS + i:NRES + STREAMS + i + 1], y_weighed)

                def mix_weight(t, i, j):
                    return kern[:, t * NRES + i * STREAMS + j:][:, 0:1]

                def diagonal(n, j):
                    t, i = END_TENSOR[n]
                    weigh(end_diagonal[:, n, j * P:(j + 1) * P], ident[:],
                          mix_weight(t, i, j), diagonal_ready)

                def term(t, j):
                    if j == 0:
                        act.wait_ge(base_added, (t + 1) * STREAMS)
                    weigh(end_term[:, j, t, :], end_c[:, j, t, :], mix_weight(t, 3, j),
                          terms_ready)

                def copy_sum(n):
                    t, i = END_TENSOR[n]
                    act.wait_ge(summed, n + 1)
                    nc.scalar.activation(end_out[:, t * STREAMS + i, :], end_bank[n][:], ACT.Copy
                                         ).then_inc(summed_copied, 1)

                act.wait_ge(acc_done, job + TILES)
                nc.scalar.activation(cond[:, 1, STREAMS - 1, TILES - 1, :], acc[TILES - 1][:],
                                     ACT.Copy).then_inc(cond_ready, 1)
                for k in range(C // P):
                    act.wait_ge(turn_done, job + k + 1)
                    if k == 1:
                        act.wait_ge(y_ready, first_tile)
                    else:
                        act.wait_ge(project_done, job + max(0, k - 1))
                    nc.scalar.activation((cond_t, xpre_t)[k % 2][:, 0, :],
                                         (turn_ps, y_ps[0])[k % 2][:], ACT.Copy
                                         ).then_inc(cond_hi_ready, 1)
                    if k == 1:
                        act.wait_ge(cond_ready, job + TILES)
                        nc.scalar.activation(acc[TILES - 1][:], acc[TILES - 1][:], ACT.Square,
                                             accum_out=ssq[:, TILES - 1, STREAMS - 1:STREAMS]
                                             ).then_inc(acc_free, 1)
                answer_rms(asks, dones)
                copy_logits(b)
                answer_softmaxes(asks)
                answer_log_step(asks, 0)
                act.wait_ge(mixed, 1 + c * MIX_PAIRS)
                weigh_streams(0)
                for t in range(TILES):
                    if t + 1 < TILES:
                        weigh_streams(t + 1)
                    split_pre(t)
                    if t > 0:
                        weigh_y(t - 1)
                weigh_y(TILES - 1)
                answer_log_step(asks, 1)
                act.wait_ge(matrix_ready, 1)
                for n in range(len(END_TENSOR)):
                    for j in range(STREAMS):
                        diagonal(n, j)
                        if n * STREAMS + j < END_GPSIMD_TERMS:
                            term(n, j)
                    if n > 0:
                        copy_sum(n - 1)
                copy_sum(len(END_TENSOR) - 1)

            def split_turned(job):
                act.wait_ge(turn_done, job + 1)
                if not (isinstance(job, int) and job == 0):
                    act.wait_ge(project_done, job)
                nc.scalar.activation(cond_t[:, 0, :], turn_ps[:], ACT.Copy
                                     ).then_inc(cond_hi_ready, 1)

            def answer(asked, o, i, func, scale=1.0):
                act.wait_ge(act_ask, asked)
                nc.scalar.activation(o, i, func, scale=scale).then_inc(act_done, 1)

            def copy_logits(b):
                act.wait_ge(project_done, b * STREAMS * TILES)
                nc.scalar.activation(xpre[0:2 * NLOGIT, :], logit_ps[0:2 * NLOGIT, :],
                                     ACT.Copy).then_inc(logit_copied, 1)

            def answer_rms(asks, dones):
                answer(asks + 1, vec[:, 1, 0:TILES], vec[:, 0, 0:TILES], ACT.Ln)
                act.wait_ge(act_done, dones + 1)
                nc.scalar.activation(vec[:, 2, 0:TILES], vec[:, 1, 0:TILES], ACT.Exp,
                                     scale=-0.5).then_inc(act_done, 1)

            def answer_softmaxes(asks):
                heads = logit[:, :, NRES:NLOGIT]
                answer(asks + 2, heads, heads, ACT.Exp)

            def answer_log_step(asks, k):
                ask = asks + (3 if k == 0 else 6)
                if k > 0:
                    answer(ask, vec[:, LOG, :], vec[:, SUM, :], ACT.Ln)
                    ask = ask + 1
                answer(ask, work[:], work[:], ACT.Exp)
                answer(ask + 1, vec[:, LOG, :], vec[:, SUM, :], ACT.Ln)
                answer(ask + 2, work[:], work[:], ACT.Exp)

            def body(b, parity, end):
                last = isinstance(b, int) and b == BATCHES - 1
                if not end:
                    for u in range(FIRST_X):
                        x_high(b, u)
                        if u < AHEAD:
                            w_high(b, u)
                asks, dones = (b - 1) * ASKS, (b - 1) * DONES
                for U in range(UNITS):
                    n, u = divmod(U, PASS_UNITS)
                    if u == 0 and (n > 0 or end):
                        tile_of_previous_pass(b, parity, n, TILES - 1)
                    if U + AHEAD < UNITS:
                        w_high(b, U + AHEAD)
                    elif not last:
                        w_high(b + 1, U + AHEAD - UNITS)
                    for k in turned_jobs(SPLIT_AT, n, u):
                        if n > 0 or end:
                            split_turned((b * STREAMS + n - 1) * TILES + k)
                    if end and U == RMS_AT:
                        answer_rms(asks, dones)
                    if end and U == STATS_AT - 1:
                        copy_logits(b)
                    if end and U < 2:
                        x_high(b, PASS_UNITS - 2 + U)
                    if not last and U >= 3 * PASS_UNITS + 2:
                        x_high(b + 1, U - 3 * PASS_UNITS - 2)
                    if not end and U + AHEAD in range(FIRST_X, PASS_UNITS):
                        x_high(b, U + AHEAD)
                    if not end and U == CONSTANTS_AT:
                        act.wait_ge(wall_in, 16)
                        nc.scalar.activation(wall_sb[:, :, 0:NLOGIT], wall_raw, ACT.Copy
                                             ).then_inc(const_hi, 1)
                        act.wait_ge(wb_in, 16)
                        nc.scalar.activation(wb_sb[:, 0, :, :], wb_raw, ACT.Copy
                                             ).then_inc(const_hi, 1)
                        act.wait_ge(base_in, 16)
                        nc.scalar.activation(gate[:, 0:1], base_sb[:, GATE:GATE + 1], ACT.Exp,
                                             scale=-1.0).then_inc(gate_exp, 1)
                    if end and U == STATS_AT:
                        answer_softmaxes(asks)
                    if end and U in BLOCK_AT:
                        answer_log_step(asks, BLOCK_AT.index(U))
                    for t in range(TILES):
                        if end and U == PRE_SPLIT_AT[t]:
                            act.wait_ge(pre_turned, (b - 1) * TILES + t + 1)
                            if t > 0:
                                act.wait_ge(y_ready, (b - 1) * TILES + t)
                            nc.scalar.activation(xpre_t[:, 0, :], y_ps[t % 2][:], ACT.Copy
                                                 ).then_inc(pre_hi_ready, 1)
                    if u == PASS_UNITS - 1:
                        for t in range(TILES - 1):
                            evacuate(b, parity, n, t)

            batches(act, body, ending)

        @block.vector
        def _(dve):
            def w_low(b, unit):
                dve.wait_ge(w_hi_ready, b * UNITS + unit + 1)
                lo, hi = unit % LO_SLOTS, unit % HI_SLOTS
                nc.vector.tensor_tensor(w_lo[:, lo, :, :], w_raw[:, lo, :, :],
                                        w_hi[:, hi, :, :].bitcast(F32), ALU.subtract
                                        ).then_inc(w_lo_vector, 1)

            def x_low(b, u):
                dve.wait_ge(x_hi_ready, b * PASS_UNITS + u + 1)
                ks = slice(2 * u, 2 * u + 2)
                nc.vector.tensor_tensor(x_lo[:, ks, :], x_raw[:, ks, :],
                                        x_hi[:, ks, :].bitcast(F32), ALU.subtract
                                        ).then_inc(x_lo_ready, 1)

            def constants():
                dve.wait_ge(const_hi, 2)
                nc.vector.tensor_tensor(wall_sb[:, :, NLOGIT:2 * NLOGIT], wall_raw,
                                        wall_sb[:, :, 0:NLOGIT].bitcast(F32), ALU.subtract
                                        ).then_inc(const_ready, 1)
                nc.vector.tensor_tensor(wb_sb[:, 1, :, :], wb_raw,
                                        wb_sb[:, 0, :, :].bitcast(F32), ALU.subtract
                                        ).then_inc(const_ready, 1)
                dve.wait_ge(ident_ready, 1)
                nc.vector.tensor_tensor(pair_sum[:], ident[0:2 * NLOGIT, 0:NLOGIT],
                                        ident[0:2 * NLOGIT, NLOGIT:2 * NLOGIT], ALU.add
                                        ).then_inc(const_ready, 1)
                dve.wait_ge(gate_exp, 1)
                nc.vector.tensor_scalar(gate[:, 1:2], gate[:, 0:1], 1.0, None, ALU.add
                                        ).then_inc(gate_ready, 1)
                dve.wait_ge(gate_ready, 1)
                nc.vector.reciprocal(gate[:, 1:2], gate[:, 1:2]).then_inc(gate_ready, 1)
                dve.wait_ge(gate_ready, 2)
                nc.vector.tensor_scalar(gate[:, 2:3], gate[:, 1:2], -1.0, 1.0, ALU.mult,
                                        ALU.add).then_inc(mixed, 1)
                dve.wait_ge(mixed, 1)

            def turned_low(job):
                dve.wait_ge(cond_hi_ready, job + 1)
                nc.vector.tensor_tensor(cond_t[:, 1, :], turn_ps[:],
                                        cond_t[:, 0, :].bitcast(F32), ALU.subtract
                                        ).then_inc(cond_lo_ready, 1)

            def body(b, parity, end, alone=False):
                first = not end
                last = isinstance(b, int) and b == BATCHES - 1
                c = b - 1
                count = [0]

                def mark(ins):
                    ins.then_inc(step, 1)
                    count[0] += 1
                    return count[0]

                def after(number):
                    dve.wait_ge(step, c * DVE_STEPS + number)

                def link(ins):
                    after(mark(ins))

                asked = [0, 0]

                def ask(ins, dones=1):
                    ins.then_inc(act_ask, 1)
                    asked[1] += dones
                    dve.wait_ge(act_done, c * DONES + asked[1])

                tt, reduce = nc.vector.tensor_tensor, nc.vector.tensor_reduce
                by_row = "p (t i j) -> p t i j"
                work_r = work[:].rearrange(by_row, i=STREAMS, j=STREAMS)
                work_c = work[:].rearrange("p (t i j) -> p t j i", i=STREAMS, j=STREAMS)
                kern_r = kern[:].rearrange(by_row, i=STREAMS, j=STREAMS)
                kern_c = kern[:].rearrange("p (t i j) -> p t j i", i=STREAMS, j=STREAMS)
                z_r = logit[:, :, 0:NRES].rearrange("p t (i j) -> p t i j", j=STREAMS)

                heads = logit[:, :, NRES:NLOGIT].rearrange("p t (h j) -> p t h j", j=STREAMS)
                head = vec[:, A, 0:2 * TILES].rearrange("p (t h) -> p t h", h=2)
                head_b = head.unsqueeze(3).to_broadcast([P, TILES, 2, STREAMS])

                def small(k):
                    return vec[:, k, :].rearrange("p (t i) -> p t i", i=STREAMS)

                def over_rows(k):
                    return small(k).unsqueeze(3).to_broadcast([P, TILES, STREAMS, STREAMS])

                def over_columns(k):
                    return small(k).unsqueeze(2).to_broadcast([P, TILES, STREAMS, STREAMS])

                def mean_square():
                    dve.wait_ge(acc_free, b * STREAMS * TILES)
                    link(reduce(vec[:, 0, 0:TILES], ssq[:], AX, ALU.add))
                    nc.vector.tensor_scalar(vec[:, 0, 0:TILES], vec[:, 0, 0:TILES], 1.0 / DIM,
                                            RMS_EPS, ALU.mult, ALU.add).then_inc(act_ask, 1)
                    asked[1] += 2

                def statistics():
                    dve.wait_ge(act_done, c * DONES + asked[1])
                    ms, r0, t = vec[:, 0, 0:TILES], vec[:, 2, 0:TILES], vec[:, 4, 0:TILES]
                    link(tt(t, r0, r0, ALU.mult))
                    link(tt(t, t, ms, ALU.mult))
                    link(nc.vector.tensor_scalar(t, t, -0.5, 1.5, ALU.mult, ALU.add))
                    link(tt(vec[:, 5, 0:TILES], r0, t, ALU.mult))
                    dve.wait_ge(logit_gathered, b)
                    tt(logit[:], turn_ps[:, 0:TILES * NLOGIT].rearrange(
                        "p (t l) -> p t l", l=NLOGIT),
                       vec[:, 5, 0:TILES].unsqueeze(2).to_broadcast([P, TILES, NLOGIT]),
                       ALU.mult).then_inc(stats_read, 1)
                    dve.wait_ge(stats_read, b)
                    link(tt(logit[:], logit[:],
                            base_sb[:, 0:NLOGIT].unsqueeze(1).to_broadcast([P, TILES, NLOGIT]),
                            ALU.add))
                    link(reduce(head, heads, AX, ALU.max))
                    tt(heads, heads, head_b, ALU.subtract).then_inc(act_ask, 1)
                    asked[1] += 1
                    z = logit[:, :, 0:NRES]
                    link(nc.vector.tensor_scalar(z, z, 1.0 / TAU, None, ALU.mult))

                def softmaxes():
                    dve.wait_ge(act_done, c * DONES + asked[1] - 1)
                    link(reduce(head, heads, AX, ALU.add))
                    link(nc.vector.reciprocal(vec[:, A, 0:2 * TILES], vec[:, A, 0:2 * TILES]))
                    link(tt(heads, heads, head_b, ALU.mult))

                def log_step(k):
                    if k == 0:
                        source = z_r
                    else:
                        ask(tt(vec[:, SUM, :], vec[:, B, :], vec[:, INV, :], ALU.mult))
                        link(tt(vec[:, COLMAX, :], vec[:, LOG, :], vec[:, COLMAX, :],
                                ALU.subtract))
                        link(tt(work_r, z_r, over_columns(COLMAX), ALU.add))
                        source = work_r
                    link(reduce(small(ROWMAX), source, AX, ALU.max))
                    tt(work_r, source, over_rows(ROWMAX), ALU.subtract).then_inc(act_ask, 1)
                    asked[1] += 1
                    if k == 0:
                        softmaxes()
                    dve.wait_ge(act_done, c * DONES + asked[1])
                    ask(reduce(small(SUM), work_r, AX, ALU.add))
                    link(tt(vec[:, ROWMAX, :], vec[:, ROWMAX, :], vec[:, LOG, :], ALU.add))
                    link(tt(work_r, z_r, over_rows(ROWMAX), ALU.subtract))
                    link(reduce(small(COLMAX), work_c, AX, ALU.max))
                    ask(tt(work_r, work_r, over_columns(COLMAX), ALU.subtract))
                    link(reduce(small(INV), work_c, AX, ALU.add))
                    link(nc.vector.reciprocal(vec[:, INV, :], vec[:, INV, :]))
                    link(tt(kern_r, work_r, over_columns(INV), ALU.mult))
                    link(tt(work_r, work_r, over_columns(INV), ALU.mult))

                def fast_step():
                    link(reduce(small(A), work_r, AX, ALU.add))
                    link(nc.vector.reciprocal(vec[:, A, :], vec[:, A, :]))
                    link(tt(work_r, kern_r, over_rows(A), ALU.mult))
                    link(reduce(small(B), work_c, AX, ALU.add))
                    link(nc.vector.reciprocal(vec[:, B, :], vec[:, B, :]))
                    link(tt(work_r, kern_r, over_columns(B), ALU.mult))

                def fast_steps_in_halves():
                    written = [count[0], count[0]]
                    for _ in range(FAST):
                        for k, work_of, over in ((A, work_r, over_rows),
                                                 (B, work_c, over_columns)):
                            for part in range(3):
                                for h in range(2):
                                    ts = slice(h * TILES // 2, (h + 1) * TILES // 2)
                                    sums = small(k)[:, ts]
                                    after(written[h])
                                    if part == 0:
                                        ins = reduce(sums, work_of[:, ts], AX, ALU.add)
                                    elif part == 1:
                                        ins = nc.vector.reciprocal(sums, sums)
                                    else:
                                        ins = tt(work_r[:, ts], kern_r[:, ts], over(k)[:, ts],
                                                 ALU.mult)
                                    written[h] = mark(ins)
                    after(written[1])

                def final_matrix():
                    link(tt(kern_r, work_r, over_rows(A), ALU.mult))
                    link(nc.vector.tensor_scalar(kern[:], kern[:], gate[:, 1:2], None, ALU.mult))
                    diagonal = kern[:].rearrange("p (t f) -> p t f", f=NRES)[
                        :, :, 0:NRES:STREAMS + 1]
                    ins = nc.vector.tensor_scalar(diagonal, diagonal, gate[:, 2:3], None, ALU.add)
                    if not alone:
                        link(ins)
                    else:
                        ins.then_inc(matrix_ready, 1)
                        dve.wait_ge(matrix_ready, 1)

                def pre(t):
                    if t > 0:
                        dve.wait_ge(pre_turned, c * TILES + t)
                    for j in range(STREAMS):
                        weight = logit[:, t, NRES + j:NRES + j + 1]
                        source = cond[:, 1 - parity, j, t, :]
                        if j == 0:
                            link(nc.vector.tensor_scalar(xpre[:], source, weight, None, ALU.mult))
                            continue
                        ins = nc.vector.scalar_tensor_tensor(
                            out=xpre[:], in0=source, scalar=weight, in1=xpre[:],
                            op0=ALU.mult, op1=ALU.add)
                        if j < STREAMS - 1:
                            link(ins)
                        else:
                            ins.then_inc(pre_ready, 1)

                def pre_low(t):
                    dve.wait_ge(pre_hi_ready, c * TILES + t + 1)
                    nc.vector.tensor_tensor(xpre_t[:, 1, :], y_ps[t % 2][:],
                                            xpre_t[:, 0, :].bitcast(F32), ALU.subtract
                                            ).then_inc(pre_lo_ready, 1)

                def mix(t, p):
                    q = 2 * t + p
                    slot = q % OUT_SLOTS
                    dve.wait_ge(residual_in[slot], (c * 2 + q // OUT_SLOTS + 1) * 16)
                    written = [0, 0]
                    for j in range(STREAMS + 1):
                        for s in range(2):
                            i = 2 * p + s
                            if j < STREAMS:
                                source = cond[:, 1 - parity, j, t, :]
                                weight = kern[:, t * NRES + i * STREAMS + j:][:, 0:1]
                            else:
                                source = y_ps[t % 2][:]
                                weight = logit[:, t, NRES + STREAMS + i:][:, 0:1]
                                if s == 0:
                                    dve.wait_ge(y_ready, c * TILES + t + 1)
                            if j > 0:
                                after(written[s])
                            ins = nc.vector.scalar_tensor_tensor(
                                out=piece[:, slot, s, :], in0=source, scalar=weight,
                                in1=piece[:, slot, s, :], op0=ALU.mult, op1=ALU.add)
                            if j == STREAMS and s == 1:
                                ins.then_inc(mixed, 1)
                            else:
                                written[s] = mark(ins)

                def share_ending():
                    for k in range(C // P):
                        job = (BATCHES * STREAMS - 1) * TILES + k
                        parts = (cond_t, xpre_t)[k % 2]
                        dve.wait_ge(cond_hi_ready, job + 1)
                        nc.vector.tensor_tensor(parts[:, 1, :], (turn_ps, y_ps[0])[k % 2][:],
                                                parts[:, 0, :].bitcast(F32), ALU.subtract
                                                ).then_inc(cond_lo_ready, 1)
                        if k == 2:
                            mean_square()
                    statistics()
                    for k in range(BLOCKS):
                        log_step(k)
                        fast_steps_in_halves()
                    final_matrix()

                    def add_term(t, i, j):
                        plane = end_out[:, t * STREAMS + i, :]
                        return nc.vector.scalar_tensor_tensor(
                            out=plane, in0=end_c[:, j, t, :],
                            scalar=kern[:, t * NRES + i * STREAMS + j:][:, 0:1],
                            in1=plane, op0=ALU.mult, op1=ALU.add)

                    for group in END_VECTOR:
                        dve.wait_ge(base_added, max(t * STREAMS + i for t, i in group) + 1)
                        written = {}
                        for j in range(STREAMS):
                            for stream in group:
                                if j > 0:
                                    after(written[stream])
                                ins = add_term(*stream, j)
                                if j == STREAMS - 1 and stream == group[-1]:
                                    ins.then_inc(mixed, 1)
                                else:
                                    written[stream] = mark(ins)
                    dve.wait_ge(terms_added, END_GPSIMD_TERMS)
                    for k in range(END_GPSIMD_TERMS, TILES * STREAMS):
                        ins = add_term(TILES - 1, STREAMS - 1, k % STREAMS)
                        if k < TILES * STREAMS - 1:
                            link(ins)
                        else:
                            ins.then_inc(mixed, 1)

                if alone:
                    share_ending()
                    return
                if first:
                    for u in range(FIRST_X):
                        x_low(b, u)
                        if u < AHEAD:
                            w_low(b, u)
                for U in range(UNITS):
                    n, u = divmod(U, PASS_UNITS)
                    if U + AHEAD in VECTOR_SUBS:
                        w_low(b, U + AHEAD)
                    if not last and U + AHEAD >= UNITS:
                        w_low(b + 1, U + AHEAD - UNITS)
                    if first and U + AHEAD in range(FIRST_X, PASS_UNITS):
                        x_low(b, U + AHEAD)
                    if first and U == CONSTANTS_AT:
                        constants()
                    for k in turned_jobs(SPLIT_AT, n, u):
                        if n > 0 or end:
                            turned_low((b * STREAMS + n - 1) * TILES + k)
                    if not end:
                        continue
                    if U == RMS_AT:
                        mean_square()
                    if U == STATS_AT:
                        statistics()
                    for t in range(TILES):
                        if U == PRE_SPLIT_AT[t]:
                            pre_low(t)
                    for k in range(BLOCKS):
                        if U == BLOCK_AT[k]:
                            log_step(k)
                        start, stop = FAST_AT[k]
                        if start <= U < stop:
                            for _ in range(FAST * (U - start) // (stop - start),
                                           FAST * (U + 1 - start) // (stop - start)):
                                fast_step()
                    if U == FINAL_AT:
                        final_matrix()
                    for q in range(MIX_PAIRS):
                        if U == MIX_AT[q]:
                            mix(q // 2, q % 2)
                    for t in range(TILES):
                        if U == PRE_AT[t]:
                            pre(t)
                if end:
                    assert count[0] == DVE_STEPS, count[0]

            batches(dve, body, lambda: body(BATCHES, 0, True, alone=True))

        @block.tensor
        def _(pe):
            def half_unit(b, U, half):
                n, u = divmod(U, PASS_UNITS)
                if half:
                    pass
                elif U in VECTOR_SUBS:
                    pe.wait_ge(w_lo_vector, b * VS + VECTOR_SUBS.index(U) + 1)
                else:
                    pe.wait_ge(w_lo_gpsimd, b * GS + GPSIMD_SUBS.index(U) + 1)
                if n == 0 and not half:
                    pe.wait_ge(x_lo_ready, b * PASS_UNITS + u + 1)
                for t in range(half * TILES // 2, (half + 1) * TILES // 2):
                    if u == 0 and not (n == 0 and isinstance(b, int) and b == 0):
                        pe.wait_ge(acc_free, (b * STREAMS + n - 1) * TILES + t + 1)
                    rows = slice(t * P, (t + 1) * P)
                    for k in range(UNIT_CHUNKS):
                        chunk = UNIT_CHUNKS * u + k
                        wh, wl = w_hi[:, U % HI_SLOTS, k, :], w_lo[:, U % LO_SLOTS, k, :]
                        xh, xl = x_hi[:, chunk, rows], x_lo[:, chunk, rows]
                        for m, (stationary, moving) in enumerate(((xh, wh), (xh, wl), (xl, wh))):
                            mm = nc.tensor.matmul(acc[t][:], stationary, moving,
                                                  start=(chunk == 0 and m == 0),
                                                  stop=(chunk == CHUNKS - 1 and m == 2))
                    if u == PASS_UNITS - 1:
                        mm.then_inc(acc_done, 1)
                if half and u < PASS_UNITS - 1:
                    mm.then_inc(unit_done, 1)

            def turn(source, plane_job, k):
                if k == 0:
                    pe.wait_ge(cond_ready, plane_job + TILES)
                if not (isinstance(plane_job, int) and plane_job + k == 0):
                    pe.wait_ge(cond_lo_ready, plane_job + k)
                for t in range(TILES):
                    mm = nc.tensor.transpose(turn_ps[:, t * P:(t + 1) * P],
                                             source[:, t, k * P:(k + 1) * P], ident[:])
                mm.then_inc(turn_done, 1)

            def project(n, k, job, parts=cond_t):
                pe.wait_ge(cond_lo_ready, job + 1)
                chunk = n * (C // P) + k
                nc.tensor.matmul(logit_ps[0:2 * NLOGIT, :], wall_sb[:, chunk, :],
                                 parts[:, 0, :], start=(chunk == 0), stop=False,
                                 skip_group_check=True)
                mm = nc.tensor.matmul(logit_ps[0:NLOGIT, :], wall_sb[:, chunk, 0:NLOGIT],
                                      parts[:, 1, :], start=False, stop=(chunk == CHUNKS - 1),
                                      skip_group_check=True)
                mm.then_inc(project_done, 1)

            def gather(b):
                pe.wait_ge(logit_copied, b)
                for t in range(TILES):
                    mm = nc.tensor.matmul(turn_ps[:, t * NLOGIT:(t + 1) * NLOGIT],
                                          xpre[0:2 * NLOGIT, t * P:(t + 1) * P], pair_sum[:],
                                          start=True, stop=True)
                mm.then_inc(logit_gathered, 1)

            def turn_pre(c, t):
                tile = c * TILES + t
                pe.wait_ge(pre_ready, tile + 1)
                pe.wait_ge(mixed, 1 + c * MIX_PAIRS + max(0, t - 1) * 2)
                for k in range(C // P):
                    cols = slice(k * P, (k + 1) * P)
                    mm = nc.tensor.transpose(y_ps[t % 2][:, cols], xpre[:, cols], ident[:])
                mm.then_inc(pre_turned, 1)

            def branch(c, t, bank):
                pe.wait_ge(pre_lo_ready, c * TILES + t + 1)
                for k in range(C // P):
                    cols = slice(k * P, (k + 1) * P)
                    high, low = xpre_t[:, 0, cols], xpre_t[:, 1, cols]
                    for m, (stationary, half) in enumerate(((high, 0), (high, 1), (low, 0))):
                        mm = nc.tensor.matmul(bank[:], stationary, wb_sb[:, half, k, :],
                                              start=(k == 0 and m == 0),
                                              stop=(k == C // P - 1 and m == 2))
                mm.then_inc(y_ready, 1)

            def ending():
                first_tile, job = (BATCHES - 1) * TILES, (BATCHES * STREAMS - 1) * TILES

                def turn_last(k):
                    if k == 0:
                        pe.wait_ge(cond_ready, job + TILES - 1)
                    if k == 1:
                        pe.wait_ge(mixed, 1 + (BATCHES - 1) * MIX_PAIRS)
                    else:
                        pe.wait_ge(cond_lo_ready, job + max(0, k - 1))
                    for t in range(TILES):
                        if k == 0 and t == TILES - 1:
                            pe.wait_ge(cond_ready, job + TILES)
                        mm = nc.tensor.transpose((turn_ps, y_ps[0])[k % 2][:, t * P:(t + 1) * P],
                                                 end_c[:, STREAMS - 1, t, k * P:(k + 1) * P],
                                                 ident[:])
                    mm.then_inc(turn_done, 1)

                def turn_terms(t):
                    pe.wait_ge(pre_weighed, (t + 1) * STREAMS)
                    if t > 1:
                        pe.wait_ge(pre_copied, t - 1)
                    for k in range(C // P):
                        cols = slice(k * P, (k + 1) * P)
                        for j in range(STREAMS):
                            mm = nc.tensor.matmul(y_ps[t % 2][:, cols], end_term[:, j, t, cols],
                                                  ident[:], start=(j == 0),
                                                  stop=(j == STREAMS - 1))
                    mm.then_inc(pre_turned, 1)

                turn_last(0)
                for k in range(C // P):
                    if k + 1 < C // P:
                        turn_last(k + 1)
                    project(STREAMS - 1, k, job + k, (cond_t, xpre_t)[k % 2])
                gather(BATCHES)
                pe.wait_ge(acc_free, BATCHES * STREAMS * TILES)
                turn_terms(0)
                for t in range(TILES):
                    if t + 1 < TILES:
                        turn_terms(t + 1)
                    branch(BATCHES - 1, t, acc[t])
                for n, (t, i) in enumerate(END_TENSOR):
                    pe.wait_ge(base_added, (t + 1) * STREAMS)
                    nc.tensor.matmul(end_bank[n][:], ident[:], end_out[:, t * STREAMS + i, :],
                                     start=True, stop=False)
                for n, (t, i) in enumerate(END_TENSOR):
                    for j in range(STREAMS):
                        pe.wait_ge(diagonal_ready, n * STREAMS + j + 1)
                        mm = nc.tensor.matmul(end_bank[n][:],
                                              end_diagonal[:, n, j * P:(j + 1) * P],
                                              end_c[:, j, t, :], start=False,
                                              stop=(j == STREAMS - 1))
                    mm.then_inc(summed, 1)

            def body(b, parity, end):
                for H in range(2 * UNITS):
                    U, half = divmod(H, 2)
                    n = U // PASS_UNITS
                    half_unit(b, U, half)
                    if n > 0 or end:
                        job = (b * STREAMS + n - 1) * TILES
                        plane, side = (n - 1, parity) if n > 0 else (STREAMS - 1, 1 - parity)
                        at = H % (2 * PASS_UNITS)
                        for k in turned_jobs(PROJECT_AT, n, at):
                            project(plane, k, job + k)
                        for k in turned_jobs(TURN_AT, n, at):
                            if n == 1 and k == 0 and not end:
                                pe.wait_ge(const_ready, 3)
                            if n == 1 and k == 0 and end:
                                pe.wait_ge(stats_read, b)
                            turn(cond[:, side, plane, :, :], job, k)
                    if end and H == GATHER_AT:
                        gather(b)
                    for t in range(TILES):
                        if end and half and U == PRE_T_AT[t]:
                            turn_pre(b - 1, t)
                        if end and half and U == Y_AT[t]:
                            branch(b - 1, t, y_ps[t % 2])

            pe.wait_ge(ident_ready, 1)
            for _ in range(WARM_UP):
                nc.tensor.transpose(turn_ps[:, 0:P], ident[:], ident[:])
            batches(pe, body, ending)


def kernel(x, itok_B_3_7, L0_cond_weight, L0_ffn_W_res, L0_ffn_W_pre, L0_ffn_W_post,
           L0_ffn_H_res_base, L0_ffn_H_pre_base, L0_ffn_H_post_base, L0_ffn_gate, L0_ffn_W_branch):
    import concourse.bacc as bacc
    from concourse.bass_utils import run_bass_kernel_spmd

    x = np.asarray(x)
    weight = np.asarray(L0_cond_weight)
    xt = x.reshape(BATCHES, TOKENS, PASS_UNITS, UNIT_CHUNKS, P).transpose(0, 2, 4, 3, 1)
    wt = weight.reshape(ADAPTERS, STREAMS, C, PASS_UNITS, UNIT_CHUNKS, P)
    wt = wt.transpose(0, 1, 3, 5, 4, 2)
    xn = x.reshape(BATCHES, TILES, P, 2, 2 * C).transpose(0, 1, 3, 2, 4)
    wall = np.concatenate([np.asarray(w) for w in (L0_ffn_W_res, L0_ffn_W_pre, L0_ffn_W_post)])
    base = np.concatenate([np.asarray(v).reshape(-1) for v in (
        L0_ffn_H_res_base, L0_ffn_H_pre_base, L0_ffn_H_post_base, L0_ffn_gate)])
    arrays = {
        "xt": xt.reshape(BATCHES * PASS_UNITS, P, UNIT_CHUNKS * TOKENS),
        "xn": xn.reshape(BATCHES * MIX_PAIRS, P, 2 * C),
        "wt": wt.reshape(ADAPTERS * UNITS, P, UNIT_CHUNKS * C),
        "ids": np.asarray(itok_B_3_7).reshape(1, BATCHES),
        "wall": wall.reshape(NLOGIT, CHUNKS, P).transpose(2, 1, 0),
        "base": base.reshape(1, NLOGIT + 1),
        "wb": np.asarray(L0_ffn_W_branch).reshape(C // P, P, C).transpose(1, 0, 2),
    }
    arrays = {name: np.ascontiguousarray(a) for name, a in arrays.items()}
    nc = bacc.Bacc("TRN2", target_bir_lowering=False, num_devices=1)
    args = [nc.dram_tensor(name, a.shape, mybir.dt.from_np(a.dtype), kind="ExternalInput").ap()
            for name, a in arrays.items()]
    out = nc.dram_tensor("out", (BATCHES * MIX_PAIRS, P, 2 * C), F32, kind="ExternalOutput").ap()
    build(nc, *args, out)
    got = run_bass_kernel_spmd(nc, [arrays], core_ids=[0]).results[0]["out"]
    got = got.reshape(BATCHES, TILES, 2, P, 2 * C).transpose(0, 1, 3, 2, 4)
    return np.ascontiguousarray(got.reshape(BATCHES, TOKENS, DIM))
```
